# Optimizing a Trainium2 kernel written in Bass

```python
import numpy as np
import jax
import jax.numpy as jnp

def _softmax(x, axis=-1):
    return jax.nn.softmax(x, axis=axis)

def _gelu(x):
    return jax.nn.gelu(x, approximate=True)

def _silu(x):
    return jax.nn.silu(x)

def _sigmoid(x):
    return jax.nn.sigmoid(x)

def _layernorm(x, axis=-1, eps=1e-05):
    m = jnp.mean(x, axis=axis, keepdims=True)
    v = jnp.var(x, axis=axis, keepdims=True)
    return (x - m) / jnp.sqrt(v + eps)

def _scatter_add(tgt, idx, src, axis=0):
    return tgt.at[idx].add(src)

def _segment_sum(src, seg, n):
    return jax.ops.segment_sum(src, seg, n)
kernel_name = 'mk_gnn_preln_d2_gnn_r64_387b68'

def setup_inputs(seed: int=0):
    np.random.seed(seed)
    _w = jnp.asarray

    def _rec_inputs():
        import jax
        import jax.numpy as jnp
        _gk = jax.random.key(seed)
        x = -0.0005121 + 1.001 * jax.random.normal(jax.random.fold_in(_gk, 1), (100000, 64), jnp.float32)
        src = jax.random.randint(jax.random.fold_in(_gk, 2), (25000,), 0, 100000, jnp.int32)
        dst = jax.random.randint(jax.random.fold_in(_gk, 3), (25000,), 0, 100000, jnp.int32)
        _o = jnp.argsort(dst, stable=True)
        src = src[_o]
        dst = dst[_o]
        edge_attr_64 = -9.77346e-05 + 0.999888 * jax.random.normal(jax.random.fold_in(_gk, 11), (25000, 64), jnp.float32)
        return (x, src, dst, edge_attr_64)
    x, src, dst, edge_attr_64 = _rec_inputs()

    def _L0_gnn_setup():
        import jax, jax.numpy as jnp
        import numpy as np
        N, E, D, H, L = (50000, 12500, 64, 4, 2)
        DH = D // H

        def layer_norm(h, g, b, eps=1e-05):
            mu = h.mean(-1, keepdims=True)
            var = ((h - mu) ** 2).mean(-1, keepdims=True)
            return (h - mu) / jnp.sqrt(var + eps) * g + b

        def exphormer_layer(h, edge_attr, src, dst, p):
            wq, wk, we, wv, wo, bo, g1, be1, w1, b1, w2, b2, g2, be2 = p
            n = h.shape[0]
            Qh = (h @ wq).reshape(n, H, DH)
            Kh = (h @ wk).reshape(n, H, DH)
            Vh = (h @ wv).reshape(n, H, DH)
            Eh = (edge_attr @ we).reshape(-1, H, DH)
            s = jnp.sum(Kh[src] * Qh[dst] * Eh, axis=-1, keepdims=True) / np.sqrt(DH)
            score = jnp.exp(jnp.clip(s, -5.0, 5.0))
            msg = Vh[src] * score
            wV = jax.ops.segment_sum(msg, dst, num_segments=n)
            Z = jax.ops.segment_sum(score, dst, num_segments=n)
            h_attn = (wV / (Z + 1e-06)).reshape(n, D)
            h1 = layer_norm(h + (h_attn @ wo + bo), g1, be1)
            ffn = jax.nn.relu(h1 @ w1 + b1) @ w2 + b2
            return layer_norm(h1 + ffn, g2, be2)
        key = jax.random.key(seed)
        ks = jax.random.split(key, 16)
        s = 1.0 / np.sqrt(D)
        inp = {'x': jax.random.normal(ks[0], (N, D), jnp.float32), 'edge_attr': jax.random.normal(ks[1], (E, D), jnp.float32), 'edge_index': jax.random.randint(ks[2], (2, E), 0, N, jnp.int64), 'WQ': jax.random.normal(ks[3], (L, D, D), jnp.float32) * s, 'WK': jax.random.normal(ks[4], (L, D, D), jnp.float32) * s, 'WE': jax.random.normal(ks[5], (L, D, D), jnp.float32) * s, 'WV': jax.random.normal(ks[6], (L, D, D), jnp.float32) * s, 'WO': jax.random.normal(ks[7], (L, D, D), jnp.float32) * s, 'bO': jnp.zeros((L, D), jnp.float32), 'ln1_g': jnp.ones((L, D), jnp.float32), 'ln1_b': jnp.zeros((L, D), jnp.float32), 'W1': jax.random.normal(ks[8], (L, D, 2 * D), jnp.float32) * s, 'b1': jnp.zeros((L, 2 * D), jnp.float32), 'W2': jax.random.normal(ks[9], (L, 2 * D, D), jnp.float32) * (1.0 / np.sqrt(2 * D)), 'b2': jnp.zeros((L, D), jnp.float32), 'ln2_g': jnp.ones((L, D), jnp.float32), 'ln2_b': jnp.zeros((L, D), jnp.float32)}
        return inp
    _L0_gnn_all = _L0_gnn_setup()
    _L0_gnn_in = {k: v for k, v in _L0_gnn_all.items() if k in ('WQ', 'WK', 'WE', 'WV', 'WO', 'bO', 'ln1_g', 'ln1_b', 'W1', 'b1', 'W2', 'b2', 'ln2_g', 'ln2_b')}
    del _L0_gnn_all

    def _L1_gnn_setup():
        import jax, jax.numpy as jnp
        import numpy as np
        import math
        N_NODES = 100000
        D = 64
        N_EDGES = 20000
        LN_EPS = 1e-05
        key = jax.random.key(seed)
        ks = jax.random.split(key, 8)
        x = jax.random.normal(ks[0], (N_NODES, D), dtype=jnp.float32)
        edge_index = jax.random.randint(ks[1], (2, N_EDGES), 0, N_NODES, dtype=jnp.int64)
        limit = 0.1 * math.sqrt(6.0 / (D + D))
        qk_w = jax.random.uniform(ks[2], (D, D), dtype=jnp.float32, minval=-limit, maxval=limit)
        v_w = jax.random.uniform(ks[3], (D, D), dtype=jnp.float32, minval=-limit, maxval=limit)
        o_w = jax.random.uniform(ks[4], (D, D), dtype=jnp.float32, minval=-limit, maxval=limit)
        qk_b = jnp.zeros((D,), dtype=jnp.float32)
        v_b = jnp.zeros((D,), dtype=jnp.float32)
        o_b = jnp.zeros((D,), dtype=jnp.float32)
        ln_g = jnp.ones((D,), dtype=jnp.float32)
        ln_b = jnp.zeros((D,), dtype=jnp.float32)
        return {'x': x, 'edge_index': edge_index, 'qk_w': qk_w, 'qk_b': qk_b, 'v_w': v_w, 'v_b': v_b, 'o_w': o_w, 'o_b': o_b, 'ln_g': ln_g, 'ln_b': ln_b}
    _L1_gnn_all = _L1_gnn_setup()
    _L1_gnn_in = {k: v for k, v in _L1_gnn_all.items() if k in ('qk_w', 'qk_b', 'v_w', 'v_b', 'o_w', 'o_b', 'ln_g', 'ln_b')}
    del _L1_gnn_all
    return {'x': x, 'src': src, 'dst': dst, 'edge_attr_64': edge_attr_64, 'L0_gnn_WQ': _L0_gnn_in['WQ'], 'L0_gnn_WK': _L0_gnn_in['WK'], 'L0_gnn_WE': _L0_gnn_in['WE'], 'L0_gnn_WV': _L0_gnn_in['WV'], 'L0_gnn_WO': _L0_gnn_in['WO'], 'L0_gnn_bO': _L0_gnn_in['bO'], 'L0_gnn_ln1_g': _L0_gnn_in['ln1_g'], 'L0_gnn_ln1_b': _L0_gnn_in['ln1_b'], 'L0_gnn_W1': _L0_gnn_in['W1'], 'L0_gnn_b1': _L0_gnn_in['b1'], 'L0_gnn_W2': _L0_gnn_in['W2'], 'L0_gnn_b2': _L0_gnn_in['b2'], 'L0_gnn_ln2_g': _L0_gnn_in['ln2_g'], 'L0_gnn_ln2_b': _L0_gnn_in['ln2_b'], 'L1_gnn_qk_w': _L1_gnn_in['qk_w'], 'L1_gnn_qk_b': _L1_gnn_in['qk_b'], 'L1_gnn_v_w': _L1_gnn_in['v_w'], 'L1_gnn_v_b': _L1_gnn_in['v_b'], 'L1_gnn_o_w': _L1_gnn_in['o_w'], 'L1_gnn_o_b': _L1_gnn_in['o_b'], 'L1_gnn_ln_g': _L1_gnn_in['ln_g'], 'L1_gnn_ln_b': _L1_gnn_in['ln_b']}

def reference(x, src, dst, edge_attr_64, L0_gnn_WQ, L0_gnn_WK, L0_gnn_WE, L0_gnn_WV, L0_gnn_WO, L0_gnn_bO, L0_gnn_ln1_g, L0_gnn_ln1_b, L0_gnn_W1, L0_gnn_b1, L0_gnn_W2, L0_gnn_b2, L0_gnn_ln2_g, L0_gnn_ln2_b, L1_gnn_qk_w, L1_gnn_qk_b, L1_gnn_v_w, L1_gnn_v_b, L1_gnn_o_w, L1_gnn_o_b, L1_gnn_ln_g, L1_gnn_ln_b):
    import jax
    import jax.numpy as jnp

    def _L0_gnn_ref(x, edge_attr, edge_index, WQ, WK, WE, WV, WO, bO, ln1_g, ln1_b, W1, b1, W2, b2, ln2_g, ln2_b):
        import jax, jax.numpy as jnp
        import numpy as np
        N, E, D, H, L = (50000, 12500, 64, 4, 2)
        DH = D // H

        def layer_norm(h, g, b, eps=1e-05):
            mu = h.mean(-1, keepdims=True)
            var = ((h - mu) ** 2).mean(-1, keepdims=True)
            return (h - mu) / jnp.sqrt(var + eps) * g + b

        def exphormer_layer(h, edge_attr, src, dst, p):
            wq, wk, we, wv, wo, bo, g1, be1, w1, b1, w2, b2, g2, be2 = p
            n = h.shape[0]
            Qh = (h @ wq).reshape(n, H, DH)
            Kh = (h @ wk).reshape(n, H, DH)
            Vh = (h @ wv).reshape(n, H, DH)
            Eh = (edge_attr @ we).reshape(-1, H, DH)
            s = jnp.sum(Kh[src] * Qh[dst] * Eh, axis=-1, keepdims=True) / np.sqrt(DH)
            score = jnp.exp(jnp.clip(s, -5.0, 5.0))
            msg = Vh[src] * score
            wV = jax.ops.segment_sum(msg, dst, num_segments=n)
            Z = jax.ops.segment_sum(score, dst, num_segments=n)
            h_attn = (wV / (Z + 1e-06)).reshape(n, D)
            h1 = layer_norm(h + (h_attn @ wo + bo), g1, be1)
            ffn = jax.nn.relu(h1 @ w1 + b1) @ w2 + b2
            return layer_norm(h1 + ffn, g2, be2)
        src = edge_index[0]
        dst = edge_index[1]
        h = x
        for l in range(L):
            p = (WQ[l], WK[l], WE[l], WV[l], WO[l], bO[l], ln1_g[l], ln1_b[l], W1[l], b1[l], W2[l], b2[l], ln2_g[l], ln2_b[l])
            h = exphormer_layer(h, edge_attr, src, dst, p)
        return h

    def _L1_gnn_ref(x, edge_index, qk_w, qk_b, v_w, v_b, o_w, o_b, ln_g, ln_b):
        import jax, jax.numpy as jnp
        import numpy as np
        import math
        N_NODES = 100000
        D = 64
        N_EDGES = 20000
        LN_EPS = 1e-05
        n = x.shape[0]
        qk = x @ qk_w.T + qk_b
        v = x @ v_w.T + v_b
        src = edge_index[0]
        dst = edge_index[1]
        scores = jnp.sum(qk[dst] * qk[src], axis=-1) / math.sqrt(v.shape[-1])
        scores = jnp.clip(scores, -5.0, 5.0)
        seg_max = jax.ops.segment_max(scores, dst, num_segments=n)
        e = jnp.exp(scores - seg_max[dst])
        seg_sum = jax.ops.segment_sum(e, dst, num_segments=n)
        attn = e / seg_sum[dst]
        out = jax.ops.segment_sum(attn[:, None] * v[src], dst, num_segments=n)
        out = out @ o_w.T + o_b
        h = out + x
        mu = jnp.mean(h, axis=-1, keepdims=True)
        var = jnp.mean(jnp.square(h - mu), axis=-1, keepdims=True)
        h = (h - mu) * jax.lax.rsqrt(var + LN_EPS)
        return h * ln_g + ln_b
    edge_index = jnp.stack([src, dst])
    h = jnp.maximum(_layernorm(x, axis=-1), 0.0)
    x = x + _L0_gnn_ref(h, edge_attr_64, edge_index, L0_gnn_WQ, L0_gnn_WK, L0_gnn_WE, L0_gnn_WV, L0_gnn_WO, L0_gnn_bO, L0_gnn_ln1_g, L0_gnn_ln1_b, L0_gnn_W1, L0_gnn_b1, L0_gnn_W2, L0_gnn_b2, L0_gnn_ln2_g, L0_gnn_ln2_b)
    h = jnp.maximum(_layernorm(x, axis=-1), 0.0)
    x = x + _L1_gnn_ref(h, edge_index, L1_gnn_qk_w, L1_gnn_qk_b, L1_gnn_v_w, L1_gnn_v_b, L1_gnn_o_w, L1_gnn_o_b, L1_gnn_ln_g, L1_gnn_ln_b)
    return x

_drawn_inputs = setup_inputs


def setup_inputs(seed=0):
    import zlib

    import numpy as np

    out = dict(_drawn_inputs(seed))
    spreads = {'L0_gnn_bO': (0.0, 0.1),
     'L0_gnn_ln1_g': (1.0, 0.2),
     'L0_gnn_ln1_b': (0.0, 0.1),
     'L0_gnn_b1': (0.0, 0.1),
     'L0_gnn_b2': (0.0, 0.1),
     'L0_gnn_ln2_g': (1.0, 0.2),
     'L0_gnn_ln2_b': (0.0, 0.1),
     'L1_gnn_qk_b': (0.0, 0.8),
     'L1_gnn_v_b': (0.0, 0.8),
     'L1_gnn_o_b': (0.0, 0.1),
     'L1_gnn_ln_g': (1.0, 0.2),
     'L1_gnn_ln_b': (0.0, 0.1)}
    factors = {'L1_gnn_qk_w': 8.0, 'L1_gnn_v_w': 8.0, 'L1_gnn_o_w': 8.0}
    for name, (base, spread) in spreads.items():
        noise = np.random.default_rng([zlib.crc32(name.encode()), seed]).standard_normal(out[name].shape)
        drawn = base * np.exp(spread * noise) if base else spread * noise
        out[name] = jnp.asarray(drawn.astype(out[name].dtype))
    for name, factor in factors.items():
        out[name] = (out[name] * factor).astype(out[name].dtype)
    return out
```

```python
import concourse.bass as bass
from concourse import mybir
from contextlib import ExitStack

N, D, E = 100000, 64, 25000
HEADS = (4, 4, 1)
GP = 8
ROWS = 128 * GP
UNITS = -(-N // ROWS)
TAIL = (N - (UNITS - 1) * ROWS) // GP
EP, ET = 125, 200
EUNITS = ET // GP
PW = D + 4
EPS, ZEPS = 1e-5, 1e-6
FAR = 1 << 20

PHASES = [(kind, layer) for layer in range(3) for kind in ("dense", "edge", "fix")]
RAW = [(k, l) for k, l in PHASES if l != 1 and k != "fix"]


def units(phase):
    return UNITS if phase[0] == "dense" else EUNITS


class Count:

    def __init__(self, sem, phases):
        self.sem, self.base, at = sem, {}, 2
        for ph in PHASES:
            self.base[ph] = at
            at += units(ph) if ph in phases else 0

    def done(self, ph, n):
        return self.sem, self.base[ph] + n + 1

    def before(self, ph, n, back=2):
        return self.sem, self.base[ph] + n + 1 - back


class Slots:

    def __init__(self, sems, phases):
        self.sems, self.base, at = sems, {}, [0, 0]
        for ph in PHASES:
            self.base[ph] = tuple(at)
            if ph in phases:
                at = [at[h] + 16 * ((units(ph) + 1 - h) // 2) for h in range(2)]

    def done(self, ph, i, h):
        return self.sems[h], self.base[ph][h] + 16 * (i + 1)

    def before(self, ph, i, h):
        return self.sems[h], self.base[ph][h] + 16 * i


def build(nc, x, src, dst, edge_attr, WQ, WK, WE, WV, WO, bO, ln1_g, ln1_b, W1, b1, W2, b2, ln2_g, ln2_b,
          qk_w, qk_b, v_w, v_b, o_w, o_b, ln_g, ln_b, out):
    f32, i32 = mybir.dt.float32, mybir.dt.int32
    ALU, ACT, AX = mybir.AluOpType, mybir.ActivationFunctionType, mybir.AxisListType
    ctx = ExitStack()
    with ctx:
        ctx.enter_context(nc.allow_non_contiguous_dma(reason="columns of biases, and single edges"))

        def sb(name, shape, dt=f32):
            return ctx.enter_context(nc.sbuf_tensor(name, shape, dt))

        def pb(name, shape):
            return ctx.enter_context(nc.psum_tensor(name, shape, f32))

        def sem(name):
            return ctx.enter_context(nc.semaphore(name))

        def dram(name, shape):
            return nc.dram_tensor(name, shape, f32)

        normed1 = dram("normed1", [N, D])
        x1 = dram("x1", [N, D])
        ends = [dram(f"ends{l}", [EUNITS, 128, 2 * GP, D]) for l in range(3)]
        targets = [dram(f"targets{l}", [EUNITS, 128, GP, D]) for l in range(3)]
        sums = [dram(f"sums{l}", [EUNITS, 128, GP, PW]) for l in range(3)]
        table = [x, normed1, x1]
        result = [normed1, x1, out]

        ident = sb("ident", [128, 128])
        center = sb("center", [128, 128])
        first_row = sb("first_row", [128, 128])
        bias_kv = sb("bias_kv", [128, 4, 128])
        bias_q = sb("bias_q", [128, 8, 64])
        w_kv = [sb(f"w_kv{l}", [128, 128]) for l in range(3)]
        w_q = [sb(f"w_q{l}", [128, 128]) for l in range(3)]
        w_e = [sb(f"w_e{l}", [128, 128]) for l in range(2)]
        w_o = [sb(f"w_o{l}", [128, 128]) for l in range(3)]
        w_1 = [sb(f"w_1{l}", [128, 128]) for l in range(2)]
        w_2 = [sb(f"w_2{l}", [128, 64]) for l in range(2)]
        wtmp = sb("wtmp", [64, 3, 128])
        wsum = sb("wsum", [128, 8])
        vec = sb("vec", [128, 32])
        names = {}

        def col(name):
            k = names.setdefault(name, len(names))
            return vec[:, k:k + 1]

        eps_col = col("eps")

        src_i = sb("src_i", [128, ET], i32)
        dst_i = sb("dst_i", [128, ET], i32)
        prev_i = sb("prev_i", [128, 1], i32)
        next_i = sb("next_i", [128, 1], i32)
        dst_f = sb("dst_f", [128, ET])
        shift_f = sb("shift_f", [128, ET])
        far_f = sb("far_f", [128, ET])
        zero_f = sb("zero_f", [128, ET])
        cont = sb("cont", [128, ET])
        head = sb("head", [128, ET])
        gidx = sb("gidx", [128, EUNITS, 2 * GP], i32)
        sidx = sb("sidx", [128, ET], i32)
        through = sb("through", [128, PW])
        throughT = sb("throughT", [PW, 128])
        carryT = sb("carryT", [PW, 136])
        carry = sb("carry", [128, PW])

        X = sb("X", [128, 2, 2 * GP, D])
        XM = sb("XM", [128, 2, 2 * GP, D])
        SQ0 = sb("SQ0", [128, 2, 2 * GP, D])
        N0 = sb("N0", [128, 2, 2 * GP, D])
        HT = sb("HT", [128, 2, 2, 4, 128])
        SQ1 = sb("SQ1", [128, 2, GP, D])
        N1 = sb("N1", [128, 2, GP, D])
        YT = sb("YT", [128, 2, 4, 128])
        HID = sb("HID", [128, 2, 2, 4, 128])
        N2 = sb("N2", [128, 2, GP, D])
        AT = sb("AT", [128, 2, 4, 128])
        OUT = sb("OUT", [128, 2, GP, D])
        X2 = sb("X2", [128, 2, GP, D])
        EA = sb("EA", [128, 2, GP, D])
        EAT = sb("EAT", [128, 4, 128])
        QS = sb("QS", [128, GP, D])
        PR = sb("PR", [128, GP, D])
        PR2 = sb("PR2", [128, GP, D])
        SC = sb("SC", [128, 2, GP * 4])
        PAY = sb("PAY", [128, 2, GP, PW])
        S = sb("S", [128, 2, GP, PW])
        SIN = sb("SIN", [128, 2, GP, PW])
        T = sb("T", [128, 2, GP, PW])
        ZR = sb("ZR", [128, 2, 2, GP * 4])
        ATT = sb("ATT", [128, 2, GP, D])
        ATTT = sb("ATTT", [128, 2, 4, 128])
        CB = sb("CB", [128, 2, GP])
        st0 = sb("st0", [128, 2, 4, 2 * GP])
        st1 = sb("st1", [128, 2, 4, GP])
        st2 = sb("st2", [128, 2, 4, GP])
        GB = sb("GB", [128, 2, 2 * GP, D])
        IB = sb("IB", [128, 2, 2 * GP], i32)

        banks = pb("banks", [128, 8, 512])
        psT = [banks[:, 4 * h, :] for h in range(2)]
        psC = [banks[:, 4 * h + 1, :] for h in range(2)]
        psH = [banks[:, 4 * h + 2:4 * h + 4, :] for h in range(2)]
        psX = [banks[:, k, :] for k in range(3)]
        psKV = banks[:, 3:5, :].rearrange("p q (j c) -> p j q c", c=128)
        psQ, psE = banks[:, 5, :], banks[:, 6, :]

        def rows8(ap):
            return ap.rearrange("p (g d) -> p g d", d=D)

        DENSE = [("dense", l) for l in range(3)]
        EDGE = [("edge", l) for l in range(3)]
        FIX = [("fix", l) for l in range(3)]
        UPD = DENSE + FIX
        FFN = [p for p in UPD if p[1] < 2]
        BACK = [p for p in UPD if p[1] > 0]
        P1 = [p for p in UPD if p[1] == 1]
        owner = {"dve": [], "act": [], "pe": []}

        def count(eng, name, phases):
            c = Count(sem(name), phases)
            owner[eng].append(c)
            return c

        xsum = count("dve", "xsum", RAW)
        xm = count("dve", "xm", RAW)
        sq0 = count("act", "sq0", RAW)
        ss0 = count("dve", "ss0", RAW)
        lg0 = count("act", "lg0", RAW)
        r0 = count("act", "r0", RAW)
        n0 = count("dve", "n0", RAW)
        tp1 = count("pe", "tp1", UPD)
        ht = count("dve", "ht", UPD)
        c1 = count("pe", "c1", UPD)
        sq1 = count("act", "sq1", UPD)
        ss1 = count("dve", "ss1", UPD)
        lg1 = count("act", "lg1", UPD)
        r1 = count("act", "r1", UPD)
        n1 = count("dve", "n1", UPD)
        tp2 = count("pe", "tp2", UPD)
        yt = count("act", "yt", UPD)
        h1 = count("pe", "h1", FFN)
        hid = count("act", "hid", FFN)
        c2 = count("pe", "c2", FFN)
        sq2 = count("act", "sq2", FFN)
        ss2 = count("dve", "ss2", FFN)
        lg2 = count("act", "lg2", FFN)
        r2 = count("act", "r2", FFN)
        n2 = count("dve", "n2", FFN)
        tp3 = count("pe", "tp3", P1)
        at = count("act", "at", P1)
        tb = count("pe", "tb", BACK)
        res = count("dve", "res", BACK)
        fb = count("dve", "fb", FIX)
        ts = count("dve", "ts", FIX)
        ze = count("dve", "ze", FIX)
        zr = count("dve", "zr", FIX)
        att = count("dve", "att", FIX)
        tpa = count("pe", "tpa", FIX)
        attT = count("act", "attT", FIX)
        tpe = count("pe", "tpe", EDGE)
        hs = count("act", "hs", EDGE)
        hd = count("act", "hd", EDGE)
        ea = count("act", "ea", EDGE[:2])
        pq = count("pe", "pq", EDGE)
        pkv = count("pe", "pkv", EDGE)
        qs = count("act", "qs", EDGE)
        pr = count("dve", "pr", EDGE)
        pr2 = count("dve", "pr2", EDGE[:2])
        sc = count("dve", "sc", EDGE)
        cl = count("dve", "cl", EDGE)
        cl2 = count("dve", "cl2", EDGE)
        ex = count("act", "ex", EDGE)
        pv = count("dve", "pv", EDGE)
        cb = count("dve", "cb", EDGE)
        sw = count("dve", "sw", EDGE)

        def slots(name, phases):
            return Slots([sem(f"{name}{h}") for h in range(2)], phases)

        ld_x = slots("ld_x", RAW)
        ld_n = slots("ld_n", [p for p in PHASES if p not in RAW])
        ld_r = slots("ld_r", BACK)
        ld_ea = slots("ld_ea", EDGE[:2])
        ld_s = slots("ld_s", FIX)
        st_out = slots("st_out", DENSE)
        st_n = slots("st_n", [EDGE[0], EDGE[2]])
        st_s = slots("st_s", EDGE)
        sc_out = slots("sc_out", FIX)
        sweep = sem("sweep")
        gathered = [sem(f"gathered{h}") for h in range(2)]
        ends_out = [sem(f"ends_out{h}") for h in range(2)]
        idx_copied = sem("idx_copied")
        phase_end = sem("phase_end")
        w_loaded, w_ready, ones_set, prep = sem("w_loaded"), sem("w_ready"), sem("ones_set"), sem("prep")
        pool_set, passed = sem("pool_set"), sem("passed")
        w_turned, w_taken = sem("w_turned"), sem("w_taken")
        e_loaded, idx_ready = sem("e_loaded"), sem("idx_ready")
        c_turn, c_scan, c_back, c_ready = sem("c_turn"), sem("c_scan"), sem("c_back"), sem("c_ready")

        def last(ph):
            return res if ph in BACK else n2

        def leaving(ph):
            return OUT if ph in BACK else N2

        def barrier(eng, ph):
            eng.drain().then_inc(phase_end, 1)
            eng.wait_ge(phase_end, 5 * (PHASES.index(ph) + 1))

        def pairs(eng, ph, front, body):
            u = units(ph)
            count_ = (u + 1) // 2
            looped = count_ - 1 if u % 2 == 0 else count_ - 2
            front(0, (0, 1))
            with eng.Fori(0, looped) as i:
                body(i, (0, 1), (0, 1))
            for i in range(looped, count_):
                last_one = (0,) if u % 2 else (0, 1)
                now = last_one if i == count_ - 1 else (0, 1)
                nxt = () if i == count_ - 1 else last_one if i == count_ - 2 else (0, 1)
                body(i, now, nxt)

        wide = {ph: (2 if ph[0] == "edge" else 1) * GP for ph in PHASES}

        def w(eng, what):
            eng.wait_ge(*what)

        vectors = []
        for l in range(2):
            vectors += [(f"bO{l}", bO[l]), (f"g1{l}", ln1_g[l]), (f"s1{l}", ln1_b[l]), (f"b2{l}", b2[l]),
                        (f"g2{l}", ln2_g[l]), (f"s2{l}", ln2_b[l])]
        vectors += [("ob", o_b), ("vb", v_b), ("lg", ln_g), ("ls", ln_b)]
        for name, _ in vectors:
            col(name)
        for l in range(2):
            col(f"fb{l}")
            col(f"y{l}")
        col("in1")
        col("obf")
        N_W = 2 * len(vectors) + 2 + 2 * (2 * 4 + 2 + 2 + 1) + 2 * 3 + 4 + 8

        block = ctx.enter_context(nc.Block())

        @block.sync
        def _(sp):
            sp.wait_ge(ones_set, 1)
            sp.dma_start(src_i[0:EP, :], src.rearrange("(p t) -> p t", t=ET)).then_inc(e_loaded, 16)
            sp.dma_start(dst_i[0:EP, :], dst.rearrange("(p t) -> p t", t=ET)).then_inc(e_loaded, 16)
            grid = dst.rearrange("(p t) -> p t", t=ET)
            sp.dma_start(prev_i[1:EP, :], grid[0:EP - 1, ET - 1:ET]).then_inc(e_loaded, 16)
            sp.dma_start(next_i[0:EP - 1, :], grid[1:EP, 0:1]).then_inc(e_loaded, 16)
            n_w = 0

            def load(to, what):
                nonlocal n_w
                n_w += 1
                sp.dma_start(to, what).then_inc(w_loaded, 16)

            for name, v in vectors:
                for q in range(2):
                    load(col(name)[64 * q:64 * q + 64, :], v.rearrange("(p a) -> p a", a=1))
            for l in range(2):
                load(col(f"fb{l}"), b1[l].rearrange("(p a) -> p a", a=1))
                for q in range(2):
                    p = slice(64 * q, 64 * q + 64)
                    load(w_kv[l][p, 0:64], WK[l])
                    load(w_kv[l][p, 64:128], WV[l])
                    load(w_q[l][p, p], WQ[l])
                    load(w_e[l][p, p], WE[l])
                    load(w_o[l][p, p], WO[l])
                    load(w_1[l][p, :], W1[l])
                load(w_2[l][:, :], W2[l])
            for k, m in enumerate((qk_w, v_w, o_w)):
                for q in range(2):
                    load(wtmp[:, k, 64 * q:64 * q + 64], m)
            for j in range(4):
                load(bias_kv[0:1, j, 0:64], qk_b.rearrange("(a n) -> a n", a=1))
            for g in range(8):
                load(bias_q[0:1, g, :], qk_b.rearrange("(a n) -> a n", a=1))
            assert n_w == N_W, (n_w, N_W)

            def node_rows(t, n, parts=slice(0, 128)):
                m = parts.stop - parts.start
                return t[bass.ds(n * ROWS + parts.start * GP, m * GP), :].rearrange("(p g) d -> p g d", g=GP)

            def pieces(ph, n):
                if ph[0] == "dense" and isinstance(n, int) and n == UNITS - 1:
                    return [slice(0, TAIL)]
                return [slice(0, 128)]

            def load_x(ph, i, h):
                n = 2 * i + h
                w(sp, xm.before(ph, n))
                for p in pieces(ph, n):
                    if ph[0] == "dense":
                        ins = sp.dma_start(X[p, h, 0:GP, :], node_rows(table[ph[1]], n, p))
                    else:
                        ins = sp.dma_start(X[:, h, :, :], ends[ph[1]][n, :, :, :])
                    ins.then_inc(ld_x.sems[h], 16)

            def load_n(ph, i, h):
                n = 2 * i + h
                w(sp, (tpe if ph[0] == "edge" else tp1).before(ph, n))
                if ph[0] == "dense":
                    for p in pieces(ph, n):
                        sp.dma_start(N0[p, h, 0:GP, :], node_rows(normed1, n, p)).then_inc(ld_n.sems[h], 16)
                elif ph[0] == "edge":
                    sp.dma_start(N0[:, h, :, :], ends[1][n, :, :, :]).then_inc(ld_n.sems[h], 16)
                elif ph[1] == 1:
                    sp.dma_start(N0[:, h, 0:GP, :], ends[1][n, :, GP:2 * GP, :]).then_inc(ld_n.sems[h], 16)
                else:
                    sp.dma_start(N0[:, h, 0:GP, :], targets[ph[1]][n, :, :, :]).then_inc(ld_n.sems[h], 16)

            def load_r(ph, i, h):
                n = 2 * i + h
                w(sp, res.before(ph, n))
                if ph[0] == "dense":
                    for p in pieces(ph, n):
                        sp.dma_start(X2[p, h, :, :], node_rows(x if ph[1] == 1 else x1, n, p)).then_inc(ld_r.sems[h], 16)
                else:
                    sp.dma_start(X2[:, h, :, :], ends[0 if ph[1] == 1 else 2][n, :, GP:2 * GP, :]).then_inc(ld_r.sems[h], 16)

            def load_ea(ph, i, h):
                n = 2 * i + h
                w(sp, tpe.before(ph, n))
                e3 = edge_attr.rearrange("(p t) d -> p t d", t=ET)
                sp.dma_start(EA[0:EP, h, :, :], e3[:, bass.ds(n * GP, GP), :]).then_inc(ld_ea.sems[h], 16)

            def load_s(ph, i, h):
                n = 2 * i + h
                w(sp, ts.before(ph, n))
                sp.dma_start(SIN[:, h, :, :], sums[ph[1]][n, :, :, :]).then_inc(ld_s.sems[h], 16)

            def loads(ph, i, halves, ahead):
                for h in halves:
                    if ph in RAW and ahead:
                        load_x(ph, i + 1, h)
                    if ph not in RAW and not ahead:
                        load_n(ph, i, h)
                    if not ahead:
                        if ph in EDGE[:2]:
                            load_ea(ph, i, h)
                        if ph in FIX:
                            load_s(ph, i, h)

            def stores(ph, i, halves):
                for h in halves:
                    n = 2 * i + h
                    if ph[0] == "dense":
                        w(sp, last(ph).done(ph, n))
                        for p in pieces(ph, n):
                            sp.dma_start(node_rows(result[ph[1]], n, p), leaving(ph)[p, h, :, :]).then_inc(st_out.sems[h], 16)
                    elif ph[0] == "edge":
                        w(sp, sw.done(ph, n))
                        sp.dma_start(sums[ph[1]][n, :, :, :], S[:, h, :, :]).then_inc(st_s.sems[h], 16)

            def store_targets(ph, i, halves):
                for h in halves:
                    n = 2 * i + h
                    w(sp, n0.done(ph, n))
                    sp.dma_start(targets[ph[1]][n, :, :, :], N0[:, h, GP:2 * GP, :]).then_inc(st_n.sems[h], 16)

            def run(ph):
                u = units(ph)
                both = (0, 1)
                pair_n = (u + 1) // 2
                end = (0,) if u % 2 else both

                def halves(i):
                    return both if not isinstance(i, int) or i < pair_n - 1 else end if i == pair_n - 1 else ()

                if ph in RAW:
                    for h in both:
                        load_x(ph, 0, h)
                loads(ph, 0, both, False)
                if ph in BACK:
                    for h in both:
                        load_r(ph, 0, h)
                if ph in RAW:
                    for h in halves(1):
                        load_x(ph, 1, h)
                if ph in RAW and ph[0] == "edge":
                    store_targets(ph, 0, both)

                def body(i, now, nxt, after):
                    loads(ph, i + 1, nxt, False)
                    if ph in RAW:
                        for h in after:
                            load_x(ph, i + 2, h)
                    if ph in RAW and ph[0] == "edge":
                        store_targets(ph, i + 1, nxt)
                    stores(ph, i, now)
                    if ph in BACK:
                        for h in nxt:
                            load_r(ph, i + 1, h)

                looped = pair_n - 3
                with sp.Fori(0, looped) as i:
                    body(i, both, both, both)
                for i in range(looped, pair_n):
                    body(i, halves(i), halves(i + 1), halves(i + 2))
                for slot, phases in ((st_out, DENSE), (st_n, [EDGE[0], EDGE[2]]), (st_s, EDGE)):
                    if ph in phases:
                        for h in both:
                            w(sp, slot.done(ph, (u + 1 - h) // 2 - 1, h))
                barrier(sp, ph)

            sp.wait_ge(prep, 4)
            for ph in PHASES:
                run(ph)

        @block.gpsimd
        def _(pool):
            pool.memset(ident[:, :], 0.0).then_inc(pool_set, 1)
            pool.wait_ge(pool_set, 1)
            pool.affine_select(out=ident[:, :], in_=ident[:, :], compare_op=ALU.not_equal, fill=1.0,
                               base=0, pattern=[[-1, 128]], channel_multiplier=1).then_inc(pool_set, 1)
            pool.wait_ge(idx_ready, 1)
            pool.drain().then_inc(prep, 1)

            def hold(sem_, value):
                pool.wait_ge(sem_, value)
                pool.sem_inc(passed, 1)

            def gather(l):
                before = l * EUNITS

                def fetch(u, h, k):
                    if l or not (isinstance(k, int) and k == 0):
                        hold(ends_out[h], 16 * (k + l * ((EUNITS + 1 - h) // 2)))
                    pool.tensor_copy(IB[:, h, :], gidx[:, bass.ds(u, 1), :].rearrange("p a k -> p (a k)")).then_inc(idx_copied, 1)
                    hold(idx_copied, idx_base[0] + u + 1)
                    for g in range(2 * GP):
                        pool.indirect_dma_start(out=GB[:, h, g, :], out_offset=None, in_=table[l][:, :],
                                                in_offset=bass.IndirectOffsetOnAxis(ap=IB[:, h, g:g + 1], axis=0)
                                                ).then_inc(gathered[h], 16)

                def put(u, h, k):
                    hold(gathered[h], 16 * 2 * GP * (k + 1 + l * ((EUNITS + 1 - h) // 2)))
                    pool.dma_start(ends[l][u, :, :, :], GB[:, h, :, :]).then_inc(ends_out[h], 16)

                fetch(0, 0, 0)
                with pool.Fori(0, EUNITS // 2) as i:
                    fetch(2 * i + 1, 1, i)
                    put(2 * i, 0, i)
                    fetch(2 * i + 2, 0, i + 1)
                    put(2 * i + 1, 1, i)
                put(EUNITS - 1, 0, EUNITS // 2)
                idx_base[0] += EUNITS
                for h in range(2):
                    pool.wait_ge(ends_out[h], 16 * (l + 1) * ((EUNITS + 1 - h) // 2))

            idx_base = [0]

            def scatter(ph):
                def one(i, h):
                    n = 2 * i + h
                    hold(sc_out.sems[h], GP * sc_out.base[ph][h] + 16 * GP * i)
                    pool.tensor_copy(IB[:, h, 0:GP], sidx[:, bass.ds(n * GP, GP)]).then_inc(idx_copied, 1)
                    hold(idx_copied, idx_base[0] + n + 1)
                    hold(*last(ph).done(ph, n))
                    for g in range(GP):
                        pool.indirect_dma_start(out=result[ph[1]][:, :],
                                                out_offset=bass.IndirectOffsetOnAxis(ap=IB[:, h, g:g + 1], axis=0),
                                                in_=leaving(ph)[:, h, g, :], in_offset=None,
                                                bounds_check=N - 1, oob_is_err=False).then_inc(sc_out.sems[h], 16)

                with pool.Fori(0, EUNITS // 2) as i:
                    one(i, 0)
                    one(i, 1)
                one(EUNITS // 2, 0)
                idx_base[0] += EUNITS
                for h in range(2):
                    pool.wait_ge(sc_out.sems[h], GP * (sc_out.base[ph][h] + 16 * ((EUNITS + 1 - h) // 2)))

            pool.wait_ge(prep, 4)
            for ph in PHASES:
                if ph[0] == "dense":
                    gather(ph[1])
                if ph[0] == "fix":
                    scatter(ph)
                barrier(pool, ph)

        @block.scalar
        def _(act):
            for c in owner["act"]:
                act.sem_inc(c.sem, 2)
            act.drain().then_inc(prep, 1)
            act.wait_ge(prep, 4)

            def square0(ph, i, h):
                n, g = 2 * i + h, wide[ph]
                w(act, xm.done(ph, n))
                act.activation(SQ0[:, h, 0:g, :], XM[:, h, 0:g, :], ACT.Square).then_inc(sq0.sem, 1)

            def rstd(ph, i, h, st, g, ss, lg, r):
                n = 2 * i + h
                w(act, ss.done(ph, n))
                act.activation(st[:, h, 2, 0:g], st[:, h, 1, 0:g], ACT.Ln, bias=eps_col, scale=1.0 / D).then_inc(lg.sem, 1)
                w(act, lg.done(ph, n))
                act.activation(st[:, h, 3, 0:g], st[:, h, 2, 0:g], ACT.Exp, scale=-0.5).then_inc(r.sem, 1)

            def square(ph, i, h, c, sq):
                n = 2 * i + h
                w(act, c.done(ph, n))
                act.activation(SQ1[:, h, :, :], rows8(psC[h]), ACT.Square).then_inc(sq.sem, 1)

            def y_turned(ph, i, h):
                n, l = 2 * i + h, ph[1]
                gain, shift = (col(f"g1{l}"), col(f"y{l}")) if l < 2 else (col("lg"), col("ls"))
                w(act, tp2.done(ph, n))
                if l == 2:
                    w(act, tb.before(ph, n))
                act.activation(YT[:, h, :, :].rearrange("p j n -> p (j n)"), psT[h], ACT.Identity, bias=shift, scale=gain
                               ).then_inc(yt.sem, 1)

            def hidden(ph, i, h):
                n, l = 2 * i + h, ph[1]
                w(act, h1.done(ph, n))
                act.activation(HID[:, h, :, :, :].rearrange("p q j n -> p (q j n)"),
                               psH[h].rearrange("p q n -> p (q n)"), ACT.Relu, bias=col(f"fb{l}"), scale=1.0
                               ).then_inc(hid.sem, 1)

            def a_turned(ph, i, h):
                n = 2 * i + h
                w(act, tp3.done(ph, n))
                w(act, tb.before(ph, n))
                act.activation(AT[:, h, :, :].rearrange("p j n -> p (j n)"), psT[h], ACT.Identity,
                               bias=col("s21"), scale=col("g21")).then_inc(at.sem, 1)

            def att_turned(ph, i, h):
                n = 2 * i + h
                w(act, tpa.done(ph, n))
                act.activation(ATTT[:, h, :, :].rearrange("p j n -> p (j n)"), psH[h][:, 0, :], ACT.Copy).then_inc(attT.sem, 1)

            def front_a(ph, i, h):
                if ph in RAW:
                    square0(ph, i, h)

            def front_b(ph, i, h):
                if ph in RAW:
                    rstd(ph, i, h, st0, wide[ph], ss0, lg0, r0)

            def front(ph):
                def f(i, halves):
                    for h in halves:
                        front_a(ph, i, h)
                    for h in halves:
                        front_b(ph, i, h)
                return f

            def update(ph):
                def body(i, now, nxt):
                    for h in now:
                        if ph[0] == "fix":
                            att_turned(ph, i, h)
                    for h in now:
                        square(ph, i, h, c1, sq1)
                    for h in nxt[0:1]:
                        front_a(ph, i + 1, h)
                    for h in now:
                        rstd(ph, i, h, st1, GP, ss1, lg1, r1)
                    for h in nxt[1:2]:
                        front_a(ph, i + 1, h)
                    for h in now:
                        y_turned(ph, i, h)
                    for h in nxt:
                        front_b(ph, i + 1, h)
                    if ph in FFN:
                        for h in now:
                            hidden(ph, i, h)
                        for h in now:
                            square(ph, i, h, c2, sq2)
                            rstd(ph, i, h, st2, GP, ss2, lg2, r2)
                    if ph in P1:
                        for h in now:
                            a_turned(ph, i, h)
                return body

            def edges(ph):
                l = ph[1]

                def one(i, h):
                    n = 2 * i + h
                    w(act, tpe.done(ph, n))
                    for k, s_ in ((0, hs), (1, hd)):
                        w(act, (pkv if k == 0 else pq).before(ph, n, 1))
                        to = HT[:, 0, k, :, :].rearrange("p j n -> p (j n)")
                        if l == 1:
                            act.activation(to, psX[k], ACT.Identity, bias=col("s20"), scale=col("g20")).then_inc(s_.sem, 1)
                        else:
                            act.activation(to, psX[k], ACT.Relu).then_inc(s_.sem, 1)
                    if l < 2:
                        act.activation(EAT[:, :, :].rearrange("p j n -> p (j n)"), psX[2], ACT.Copy).then_inc(ea.sem, 1)
                    w(act, pq.done(ph, n))
                    w(act, pr.before(ph, n, 1))
                    act.activation(QS[:, :, :], rows8(psQ), ACT.Copy).then_inc(qs.sem, 1)
                    w(act, cl2.done(ph, n))
                    w(act, sw.before(ph, n))
                    hh = HEADS[l]
                    act.activation(PAY[:, h, :, D:D + hh], SC[:, 1, 0:GP * hh].rearrange("p (g k) -> p g k", k=hh),
                                   ACT.Exp).then_inc(ex.sem, 1)

                def body(i, now, nxt):
                    for h in nxt:
                        front_a(ph, i + 1, h)
                    for h in now[0:1]:
                        one(i, h)
                    for h in nxt:
                        front_b(ph, i + 1, h)
                    for h in now[1:2]:
                        one(i, h)
                return body

            for ph in PHASES:
                pairs(act, ph, front(ph), edges(ph) if ph[0] == "edge" else update(ph))
                barrier(act, ph)

        @block.vector
        def _(dve):
            for c in owner["dve"]:
                dve.sem_inc(c.sem, 2)
            done = [0]

            def step(ins):
                done[0] += 1
                ins.then_inc(ones_set, 1)
                return done[0]

            def chain(ins):
                step(ins)
                dve.wait_ge(ones_set, done[0])

            for t in (dst_i, src_i):
                dve.memset(t[:, :], FAR if t is dst_i else 0)
            dve.memset(prev_i[:, :], -1)
            dve.memset(next_i[:, :], -1)
            for t in (EA, S, X, N0, X2):
                dve.memset(t[:, :, :, :], 0.0)
            for t in (first_row, vec, *w_q, *w_e, *w_o):
                dve.memset(t[:, :], 0.0)
            dve.memset(bias_kv[:, :, :], 0.0)
            dve.memset(bias_q[:, :, :], 0.0)
            dve.memset(zero_f[:, :], 0.0)
            dve.memset(carryT[:, :], 0.0)
            dve.memset(PAY[:, :, :, :], 0.0)
            chain(dve.drain())
            dve.memset(first_row[0:1, :], 1.0)
            dve.memset(eps_col, EPS)
            dve.memset(center[:, :], 0.0)
            chain(dve.drain())
            dve.memset(center[0:64, 0:64], -1.0 / D)
            dve.memset(center[64:128, 64:128], -1.0 / D)
            dve.wait_ge(pool_set, 2)
            chain(dve.drain())
            chain(dve.tensor_tensor(out=center[:, :], in0=center[:, :], in1=ident[:, :], op=ALU.add))
            dve.wait_ge(e_loaded, 64)
            chain(dve.tensor_copy(dst_f[:, :], dst_i[:, :]))
            dve.tensor_copy(shift_f[:, 1:ET], dst_f[:, 0:ET - 1])
            dve.tensor_copy(shift_f[:, 0:1], prev_i[:, :])
            chain(dve.drain())
            chain(dve.tensor_tensor(out=cont[:, :], in0=dst_f[:, :], in1=shift_f[:, :], op=ALU.is_equal))
            chain(dve.tensor_tensor_scan(out=head[:, :], data0=cont[:, :], data1=zero_f[:, :], initial=1.0,
                                         op0=ALU.mult, op1=ALU.add))
            dve.tensor_copy(through[:, :], head[:, ET - 1:ET].to_broadcast([128, PW]))
            dve.memset(cont[:, 0:1], 0.0)
            dve.tensor_copy(shift_f[:, 0:ET - 1], dst_f[:, 1:ET])
            dve.tensor_copy(shift_f[:, ET - 1:ET], next_i[:, :])
            chain(dve.drain())
            chain(dve.tensor_tensor(out=far_f[:, :], in0=dst_f[:, :], in1=shift_f[:, :], op=ALU.is_equal))
            chain(dve.scalar_tensor_tensor(out=far_f[:, :], in0=far_f[:, :], scalar=float(FAR), in1=dst_f[:, :],
                                           op0=ALU.mult, op1=ALU.add))
            dve.tensor_copy(sidx[:, :], far_f[:, :])
            dve.tensor_copy(gidx[:, :, 0:GP], src_i[:, :].rearrange("p (u g) -> p u g", g=GP))
            chain(dve.tensor_scalar(out=dst_f[:, :], in0=dst_f[:, :], scalar1=float(N - 1), scalar2=None, op0=ALU.min))
            dve.tensor_copy(gidx[:, :, GP:2 * GP], dst_f[:, :].rearrange("p (u g) -> p u g", g=GP))
            dve.drain().then_inc(idx_ready, 1)
            dve.wait_ge(w_loaded, 16 * N_W)
            dve.wait_ge(w_turned, 3)
            for q in range(2):
                p = slice(64 * q, 64 * q + 64)
                dve.tensor_copy(w_kv[2][p, 0:64], banks[p, 0, 0:64])
                dve.tensor_copy(w_kv[2][p, 64:128], banks[p, 1, 0:64])
                dve.tensor_copy(w_q[2][p, p], banks[p, 0, 0:64])
                dve.tensor_copy(w_o[2][p, p], banks[p, 2, 0:64])
            chain(dve.drain())
            dve.drain().then_inc(w_taken, 1)
            dve.wait_ge(w_turned, 6)
            for l in range(2):
                dve.tensor_tensor(out=col(f"fb{l}"), in0=col(f"fb{l}"), in1=banks[:, 4 + l, 0:1], op=ALU.subtract)
                dve.tensor_tensor(out=col(f"y{l}"), in0=col(f"s1{l}"), in1=col(f"b2{l}"), op=ALU.add)
            dve.tensor_tensor(out=col("obf"), in0=col("ob"), in1=banks[:, 6, 0:1], op=ALU.add)
            dve.tensor_tensor(out=col("in1"), in0=col("s20"), in1=col("bO1"), op=ALU.add)
            dve.tensor_copy(throughT[:, :], banks[0:PW, 7, 0:128])
            for l in range(3):
                for q in range(2):
                    p = slice(64 * q, 64 * q + 64)
                    dve.tensor_reduce(out=wsum[p, l:l + 1], in_=w_o[l][p, p], axis=AX.X, op=ALU.add)
            for l in range(2):
                dve.tensor_reduce(out=wsum[:, 3 + l:4 + l], in_=w_2[l][:, :], axis=AX.X, op=ALU.add)
            chain(dve.drain())
            chain(dve.tensor_scalar(out=wsum[:, 0:5], in0=wsum[:, 0:5], scalar1=1.0 / D, scalar2=None, op0=ALU.mult))
            for l in range(3):
                for q in range(2):
                    p = slice(64 * q, 64 * q + 64)
                    dve.tensor_scalar(out=w_o[l][p, p], in0=w_o[l][p, p], scalar1=wsum[p, l:l + 1], scalar2=None,
                                      op0=ALU.subtract)
            for l in range(2):
                dve.tensor_scalar(out=w_2[l][:, :], in0=w_2[l][:, :], scalar1=wsum[:, 3 + l:4 + l], scalar2=None,
                                  op0=ALU.subtract)
            dve.drain().then_inc(prep, 1)
            dve.wait_ge(prep, 4)

            def sum_x(ph, i, h):
                n, g = 2 * i + h, wide[ph]
                w(dve, ld_x.done(ph, i, h))
                dve.tensor_reduce(out=st0[:, h, 0, 0:g], in_=X[:, h, 0:g, :], axis=AX.X, op=ALU.add).then_inc(xsum.sem, 1)

            def centre_x(ph, i, h):
                n, g = 2 * i + h, wide[ph]
                w(dve, xsum.done(ph, n))
                dve.scalar_tensor_tensor(out=XM[:, h, 0:g, :], in0=st0[:, h, 0, 0:g].unsqueeze(2).to_broadcast([128, g, D]),
                                         scalar=-1.0 / D, in1=X[:, h, 0:g, :], op0=ALU.mult, op1=ALU.add
                                         ).then_inc(xm.sem, 1)

            def squares0(ph, i, h):
                n, g = 2 * i + h, wide[ph]
                w(dve, sq0.done(ph, n))
                dve.tensor_reduce(out=st0[:, h, 1, 0:g], in_=SQ0[:, h, 0:g, :], axis=AX.X, op=ALU.add).then_inc(ss0.sem, 1)

            def norm_x(ph, i, h):
                n, g = 2 * i + h, wide[ph]
                w(dve, r0.done(ph, n))
                w(dve, (tpe if ph[0] == "edge" else tp1).before(ph, n))
                if ph[0] == "edge":
                    w(dve, st_n.before(ph, i, h))
                dve.tensor_tensor(out=N0[:, h, 0:g, :], in0=XM[:, h, 0:g, :],
                                  in1=st0[:, h, 3, 0:g].unsqueeze(2).to_broadcast([128, g, D]), op=ALU.mult
                                  ).then_inc(n0.sem, 1)

            def h_turned(ph, i, h):
                n, l = 2 * i + h, ph[1]
                w(dve, tp1.done(ph, n))
                to = HT[:, h, 0, :, :].rearrange("p j n -> p (j n)")
                if l == 1:
                    ins = dve.tensor_scalar(out=to, in0=psT[h], scalar1=col("g20"), scalar2=col("in1"),
                                            op0=ALU.mult, op1=ALU.add)
                else:
                    bias = col("bO0") if l == 0 else col("ob") if ph[0] == "dense" else col("obf")
                    ins = dve.tensor_scalar(out=to, in0=psT[h], scalar1=0.0, scalar2=bias, op0=ALU.max, op1=ALU.add)
                ins.then_inc(ht.sem, 1)

            def squares(ph, i, h, st, sq, ss):
                n = 2 * i + h
                w(dve, sq.done(ph, n))
                dve.tensor_reduce(out=st[:, h, 1, :], in_=SQ1[:, h, :, :], axis=AX.X, op=ALU.add).then_inc(ss.sem, 1)

            def norm(ph, i, h, st, r, to, out_sem):
                n = 2 * i + h
                w(dve, r.done(ph, n))
                dve.tensor_tensor(out=to[:, h, :, :], in0=rows8(psC[h]),
                                  in1=st[:, h, 3, :].unsqueeze(2).to_broadcast([128, GP, D]), op=ALU.mult
                                  ).then_inc(out_sem.sem, 1)

            def free_out(ph, i, h):
                if ph[0] == "dense":
                    w(dve, st_out.before(ph, i, h))
                else:
                    dve.wait_ge(sc_out.sems[h], GP * sc_out.base[ph][h] + 16 * GP * i)

            def add_residual(ph, i, h):
                n = 2 * i + h
                w(dve, tb.done(ph, n))
                w(dve, ld_r.done(ph, i, h))
                free_out(ph, i, h)
                dve.tensor_tensor(out=OUT[:, h, :, :], in0=rows8(psC[h]), in1=X2[:, h, :, :], op=ALU.add).then_inc(res.sem, 1)

            def attention(ph, i, h):
                n, hh = 2 * i + h, HEADS[ph[1]]
                dve.tensor_copy(CB[:, h, :], head[:, bass.ds(n * GP, GP)]).then_inc(fb.sem, 1)
                w(dve, fb.done(ph, n))
                w(dve, ld_s.done(ph, i, h))
                for g in range(GP):
                    ins = dve.scalar_tensor_tensor(out=T[:, h, g, 0:D + hh], in0=carry[:, 0:D + hh], scalar=CB[:, h, g:g + 1],
                                                   in1=SIN[:, h, g, 0:D + hh], op0=ALU.mult, op1=ALU.add)
                ins.then_inc(ts.sem, 1)
                w(dve, ts.done(ph, n))
                z = [ZR[:, h, k, 0:GP * hh].rearrange("p (g k) -> p g k", k=hh) for k in range(2)]
                dve.tensor_scalar(out=z[0], in0=T[:, h, :, D:D + hh], scalar1=ZEPS if ph[1] < 2 else 0.0, scalar2=None,
                                  op0=ALU.add).then_inc(ze.sem, 1)
                w(dve, ze.done(ph, n))
                dve.reciprocal(out=z[1], in_=z[0]).then_inc(zr.sem, 1)
                w(dve, zr.done(ph, n))
                dve.tensor_tensor(out=ATT[:, h, :, :].rearrange("p g (k d) -> p g k d", k=hh),
                                  in0=T[:, h, :, 0:D].rearrange("p g (k d) -> p g k d", k=hh),
                                  in1=z[1].unsqueeze(3).to_broadcast([128, GP, hh, D // hh]), op=ALU.mult).then_inc(att.sem, 1)

            def front_a(ph, i, h):
                if ph in RAW:
                    sum_x(ph, i, h)
                    centre_x(ph, i, h)

            def front_b(ph, i, halves):
                if ph in RAW:
                    for h in halves:
                        squares0(ph, i, h)
                    for h in halves:
                        norm_x(ph, i, h)

            def front(ph):
                def f(i, halves):
                    for h in halves:
                        front_a(ph, i, h)
                    front_b(ph, i, halves)
                    if ph[0] == "fix":
                        for h in halves:
                            attention(ph, i, h)
                return f

            def update(ph):
                def body(i, now, nxt):
                    for h in now:
                        h_turned(ph, i, h)
                    for h in nxt[0:1]:
                        front_a(ph, i + 1, h)
                    for h in now:
                        squares(ph, i, h, st1, sq1, ss1)
                    for h in nxt[1:2]:
                        front_a(ph, i + 1, h)
                    for h in now:
                        norm(ph, i, h, st1, r1, N1, n1)
                    front_b(ph, i + 1, nxt)
                    if ph[0] == "fix":
                        for h in nxt:
                            w(dve, tpa.done(ph, 2 * i + h))
                            attention(ph, i + 1, h)
                    if ph in FFN:
                        for h in now:
                            squares(ph, i, h, st2, sq2, ss2)
                        for h in now:
                            if ph not in BACK:
                                free_out(ph, i, h)
                            norm(ph, i, h, st2, r2, N2, n2)
                    if ph in BACK:
                        for h in now:
                            add_residual(ph, i, h)
                return body

            def edges(ph):
                l = ph[1]
                hh = HEADS[l]

                def score(i, h):
                    n = 2 * i + h
                    w(dve, pkv.done(ph, n))
                    w(dve, qs.done(ph, n))
                    dve.tensor_tensor(out=PR[:, :, :].rearrange("p (j q) d -> p j q d", q=2), in0=psKV[:, :, :, 0:64],
                                      in1=QS[:, :, :].rearrange("p (j q) d -> p j q d", q=2), op=ALU.mult).then_inc(pr.sem, 1)
                    w(dve, pr.done(ph, n))
                    prod = PR
                    if l < 2:
                        prod = PR2
                        dve.tensor_tensor(out=PR2[:, :, :], in0=rows8(psE), in1=PR[:, :, :], op=ALU.mult).then_inc(pr2.sem, 1)
                        w(dve, pr2.done(ph, n))
                    dve.tensor_reduce(out=SC[:, 0, 0:GP * hh], in_=prod[:, :, :].rearrange("p g (k d) -> p (g k) d", k=hh),
                                      axis=AX.X, op=ALU.add).then_inc(sc.sem, 1)
                    w(dve, sc.done(ph, n))
                    scale = (D // hh) ** -0.5
                    dve.tensor_scalar(out=SC[:, 0, 0:GP * hh], in0=SC[:, 0, 0:GP * hh], scalar1=scale, scalar2=5.0,
                                      op0=ALU.mult, op1=ALU.min).then_inc(cl.sem, 1)
                    w(dve, cl.done(ph, n))
                    w(dve, ex.before(ph, n, 1))
                    dve.tensor_scalar(out=SC[:, 1, 0:GP * hh], in0=SC[:, 0, 0:GP * hh], scalar1=-5.0, scalar2=None,
                                      op0=ALU.max).then_inc(cl2.sem, 1)

                def message(i, h):
                    n = 2 * i + h
                    dve.tensor_copy(CB[:, h, :], cont[:, bass.ds(n * GP, GP)]).then_inc(cb.sem, 1)
                    w(dve, ex.done(ph, n))
                    for q in range(2):
                        pay = PAY[:, h, :, :].rearrange("p (j q) c -> p q j c", q=2)[:, q, :, :]
                        ins = dve.tensor_tensor(out=pay[:, :, 0:D].rearrange("p j (k d) -> p j k d", k=hh),
                                                in0=psKV[:, :, q, 64:128].rearrange("p j (k d) -> p j k d", k=hh),
                                                in1=pay[:, :, D:D + hh].unsqueeze(3).to_broadcast([128, 4, hh, D // hh]),
                                                op=ALU.mult)
                    ins.then_inc(pv.sem, 1)
                    w(dve, pv.done(ph, n))
                    w(dve, cb.done(ph, n))
                    w(dve, st_s.before(ph, i, h))
                    for g in range(GP):
                        prev = S[:, h, g - 1, 0:D + hh] if g else S[:, 1 - h, GP - 1, 0:D + hh]
                        ins = dve.scalar_tensor_tensor(out=S[:, h, g, 0:D + hh], in0=prev, scalar=CB[:, h, g:g + 1],
                                                       in1=PAY[:, h, g, 0:D + hh], op0=ALU.mult, op1=ALU.add)
                        if g < GP - 1:
                            ins.then_inc(sweep, 1)
                            dve.wait_ge(sweep, (GP - 1) * (l * EUNITS + n) + g + 1)
                    ins.then_inc(sw.sem, 1)
                    w(dve, sw.done(ph, n))

                def body(i, now, nxt):
                    for h in nxt:
                        front_a(ph, i + 1, h)
                    for h in now[0:1]:
                        score(i, h)
                        message(i, h)
                    front_b(ph, i + 1, nxt)
                    for h in now[1:2]:
                        score(i, h)
                        message(i, h)
                return body

            def carry_over(l):
                hh = HEADS[l]
                dve.wait_ge(c_turn, l + 1)
                dve.tensor_tensor_scan(out=carryT[0:D + hh, 1:129], data0=throughT[0:D + hh, :],
                                       data1=banks[0:D + hh, 0, 0:128], initial=0.0, op0=ALU.mult, op1=ALU.add
                                       ).then_inc(c_scan, 1)
                dve.wait_ge(c_back, l + 1)
                dve.tensor_copy(carry[:, 0:D + hh], banks[:, 1, 0:D + hh]).then_inc(c_ready, 1)
                dve.wait_ge(c_ready, l + 1)

            for ph in PHASES:
                if ph[0] == "fix":
                    carry_over(ph[1])
                pairs(dve, ph, front(ph), edges(ph) if ph[0] == "edge" else update(ph))
                barrier(dve, ph)

        @block.tensor
        def _(pe):
            for c in owner["pe"]:
                pe.sem_inc(c.sem, 2)
            pe.wait_ge(w_loaded, 16 * N_W)
            pe.wait_ge(pool_set, 2)
            pe.wait_ge(idx_ready, 1)
            for k in range(3):
                pe.transpose(banks[:, k, 0:64], wtmp[:, k, :], ident[0:64, 0:64]).then_inc(w_turned, 1)
            pe.wait_ge(w_taken, 1)
            for l in range(2):
                ins = pe.matmul(banks[:, 4 + l, 0:1], w_1[l][0:64, :], col(f"b2{l}")[0:64, :], start=True, stop=True)
            ins.then_inc(w_turned, 1)
            for q in range(2):
                p = slice(64 * q, 64 * q + 64)
                ins = pe.matmul(banks[p, 6, 0:1], w_o[2][:, p], col("vb"), start=True, stop=True)
            ins.then_inc(w_turned, 1)
            pe.transpose(banks[0:PW, 7, 0:128], through[:, :], ident[:, :]).then_inc(w_turned, 1)
            pe.drain().then_inc(prep, 1)
            pe.wait_ge(prep, 4)

            def turn(to, rows, h, g0=0):
                for j in range(4):
                    ins = pe.transpose(to[:, 128 * j:128 * j + 128],
                                       rows[:, h, g0 + 2 * j:g0 + 2 * j + 2, :].rearrange("p g d -> p (g d)"), ident[:, :])
                return ins

            def back_to_rows(to, turned, h):
                for j in range(4):
                    ins = pe.transpose(to[:, 128 * j:128 * j + 128], turned[:, h, j, :], ident[:, :])
                return ins

            def tp_in(ph, i, h):
                w(pe, n0.done(ph, 2 * i + h) if ph in RAW else ld_n.done(ph, i, h))
                turn(psT[h], N0, h).then_inc(tp1.sem, 1)

            def tp_att(ph, i, h):
                w(pe, att.done(ph, 2 * i + h))
                turn(psH[h][:, 0, :], ATT, h).then_inc(tpa.sem, 1)

            def centred(ph, i, h):
                n = 2 * i + h
                w(pe, ht.done(ph, n))
                if ph[0] == "fix":
                    w(pe, attT.done(ph, n))
                w(pe, last(ph).before(ph, n))
                for j in range(4):
                    to = psC[h][:, 128 * j:128 * j + 128]
                    fixed = ph[0] == "fix"
                    ins = pe.matmul(to, HT[:, h, 0, j, :], center[:, :], start=True, stop=not fixed)
                    if fixed:
                        ins = pe.matmul(to, ATTT[:, h, j, :], w_o[ph[1]][:, :], start=False, stop=True)
                ins.then_inc(c1.sem, 1)

            def tp_mid(ph, i, h):
                w(pe, n1.done(ph, 2 * i + h))
                turn(psT[h], N1, h).then_inc(tp2.sem, 1)

            def hidden(ph, i, h):
                w(pe, yt.done(ph, 2 * i + h))
                for q in range(2):
                    p = slice(64 * q, 64 * q + 64)
                    ins = pe.matmul(psH[h][:, q, :], w_1[ph[1]][p, :], YT[p, h, :, :].rearrange("p j n -> p (j n)"),
                                    start=True, stop=True)
                ins.then_inc(h1.sem, 1)

            def centred2(ph, i, h):
                w(pe, hid.done(ph, 2 * i + h))
                for j in range(4):
                    to = psC[h][:, 128 * j:128 * j + 128]
                    pe.matmul(to, YT[:, h, j, :], center[:, :], start=True, stop=True)
                    for q in range(2):
                        ins = pe.matmul(to[:, 64 * q:64 * q + 64], HID[:, h, q, j, :], w_2[ph[1]][:, :],
                                        start=False, stop=True, skip_group_check=True)
                ins.then_inc(c2.sem, 1)

            def tp_out(ph, i, h):
                w(pe, n2.done(ph, 2 * i + h))
                turn(psT[h], N2, h).then_inc(tp3.sem, 1)

            def to_rows(ph, i, h):
                n = 2 * i + h
                if ph in P1:
                    w(pe, at.done(ph, n))
                    back_to_rows(psC[h], AT, h).then_inc(tb.sem, 1)
                else:
                    w(pe, yt.done(ph, n))
                    back_to_rows(psC[h], YT, h).then_inc(tb.sem, 1)

            def update(ph):
                def body(i, now, nxt):
                    for h in now:
                        tp_in(ph, i, h)
                    if ph[0] == "fix":
                        for h in now:
                            tp_att(ph, i, h)
                    for f in (centred, tp_mid):
                        for h in now:
                            f(ph, i, h)
                    if ph in FFN:
                        for f in (hidden, centred2):
                            for h in now:
                                f(ph, i, h)
                    if ph in P1:
                        for h in now:
                            tp_out(ph, i, h)
                    if ph in BACK:
                        for h in now:
                            to_rows(ph, i, h)
                return body

            def edges(ph):
                l = ph[1]

                def one(i, h):
                    n = 2 * i + h
                    w(pe, n0.done(ph, n) if ph in RAW else ld_n.done(ph, i, h))
                    turn(psX[0], N0, h)
                    ins = turn(psX[1], N0, h, GP)
                    if l < 2:
                        w(pe, ld_ea.done(ph, i, h))
                        ins = turn(psX[2], EA, h)
                    ins.then_inc(tpe.sem, 1)
                    w(pe, hd.done(ph, n))
                    if l == 2:
                        pe.matmul(psQ, first_row[:, :], bias_q[:, :, :].rearrange("p g d -> p (g d)"), start=True, stop=True)
                    for j in range(4):
                        ins = pe.matmul(psQ[:, 128 * j:128 * j + 128], HT[:, 0, 1, j, :], w_q[l][:, :],
                                        start=l < 2, stop=True, skip_group_check=l == 2)
                    if l < 2:
                        w(pe, ea.done(ph, n))
                        w(pe, pr2.before(ph, n, 1))
                        for j in range(4):
                            ins = pe.matmul(psE[:, 128 * j:128 * j + 128], EAT[:, j, :], w_e[l][:, :], start=True, stop=True)
                    ins.then_inc(pq.sem, 1)
                    w(pe, pv.before(ph, n, 1))
                    if l == 2:
                        for q in range(2):
                            pe.matmul(banks[:, 3 + q, :], first_row[:, :], bias_kv[:, :, :].rearrange("p j c -> p (j c)"),
                                      start=True, stop=True)
                    for j in range(4):
                        for q in range(2):
                            p = slice(64 * q, 64 * q + 64)
                            ins = pe.matmul(banks[:, 3 + q, 128 * j:128 * j + 128], HT[p, 0, 0, j, :], w_kv[l][p, :],
                                            start=l < 2, stop=True, skip_group_check=l == 2)
                    ins.then_inc(pkv.sem, 1)

                def body(i, now, nxt):
                    for h in now:
                        one(i, h)
                return body

            for ph in PHASES:
                if ph[0] == "fix":
                    hh = HEADS[ph[1]]
                    pe.transpose(banks[0:D + hh, 0, 0:128], S[:, (EUNITS - 1) % 2, GP - 1, 0:D + hh], ident[:, :]).then_inc(c_turn, 1)
                    pe.wait_ge(c_scan, ph[1] + 1)
                    pe.transpose(banks[:, 1, 0:D + hh], carryT[0:D + hh, 0:128], ident[0:D + hh, 0:D + hh]).then_inc(c_back, 1)
                    pe.wait_ge(c_ready, ph[1] + 1)
                pairs(pe, ph, lambda i, halves: None, edges(ph) if ph[0] == "edge" else update(ph))
                barrier(pe, ph)


_INS = ['x', 'src', 'dst', 'edge_attr_64', 'L0_gnn_WQ', 'L0_gnn_WK', 'L0_gnn_WE', 'L0_gnn_WV', 'L0_gnn_WO', 'L0_gnn_bO',
        'L0_gnn_ln1_g', 'L0_gnn_ln1_b', 'L0_gnn_W1', 'L0_gnn_b1', 'L0_gnn_W2', 'L0_gnn_b2', 'L0_gnn_ln2_g', 'L0_gnn_ln2_b',
        'L1_gnn_qk_w', 'L1_gnn_qk_b', 'L1_gnn_v_w', 'L1_gnn_v_b', 'L1_gnn_o_w', 'L1_gnn_o_b', 'L1_gnn_ln_g', 'L1_gnn_ln_b']


def kernel(**inputs):
    import numpy as _np
    import concourse.bacc as _bacc
    from concourse import mybir as _mybir
    from concourse.bass_utils import run_bass_kernel_spmd as _run

    nc = _bacc.Bacc("TRN2", target_bir_lowering=False, num_devices=1)
    arrays, args = {}, []
    for name in _INS:
        a = _np.ascontiguousarray(inputs[name])
        arrays[f"in_{name}_dram"] = a
        args.append(nc.dram_tensor(f"in_{name}_dram", a.shape, _mybir.dt.from_np(a.dtype), kind="ExternalInput").ap())
    args.append(nc.dram_tensor("out_0_dram", (N, D), _mybir.dt.float32, kind="ExternalOutput").ap())
    build(nc, *args)
    r = _run(nc, [arrays], core_ids=[0])
    return r.results[0]["out_0_dram"]
```

```python
import concourse.bass as bass
from concourse import mybir
from contextlib import ExitStack

N, D, E = 100000, 64, 25000
HEADS = (4, 4, 1)
GP = 8
ROWS = 128 * GP
UNITS = -(-N // ROWS)
TAIL = (N - (UNITS - 1) * ROWS) // GP
EP, ET = 125, 200
EUNITS = ET // GP
PW = D + 4
EPS, ZEPS = 1e-5, 1e-6
LN_EXP_SET = 6
FAR = 1 << 20

PHASES = [(kind, layer) for layer in range(3) for kind in ("dense", "edge", "fix")]
RAW = [(k, l) for k, l in PHASES if l != 1 and k != "fix"]


def units(phase):
    return UNITS if phase[0] == "dense" else EUNITS


class Count:

    def __init__(self, sem, phases):
        self.sem, self.base, at = sem, {}, 2
        for ph in PHASES:
            self.base[ph] = at
            at += units(ph) if ph in phases else 0

    def done(self, ph, u):
        return self.sem, self.base[ph] + u.n + 1

    def before(self, ph, u, back=2):
        return self.sem, self.base[ph] + u.n + 1 - back


class Slots:

    def __init__(self, sems, phases):
        self.sems, self.base, at = sems, {}, [0, 0]
        for ph in PHASES:
            self.base[ph] = tuple(at)
            if ph in phases:
                at = [at[h] + 16 * ((units(ph) + 1 - h) // 2) for h in range(2)]

    def done(self, ph, u):
        return self.sems[u.slot], self.base[ph][u.slot] + 16 * (u.turn + 1)

    def before(self, ph, u):
        return self.sems[u.slot], self.base[ph][u.slot] + 16 * u.turn


class Unit:

    def __init__(self, pair, off):
        self.n, self.slot, self.turn = 2 * pair + off, off % 2, pair + off // 2


def periods(eng, count, lo, hi, body):
    def written(u):
        body(lambda k: [Unit(0, u + k)] if 0 <= u + k < count else [])

    first = -(lo // 2) if lo < 0 else 0
    end = max(first, (count - hi) // 2)
    for u in range(-hi, 2 * first):
        written(u)
    if end - first > 1:
        with eng.Fori(first, end) as i:
            for s in range(2):
                body(lambda k, s=s: [Unit(i, s + k)])
    else:
        end = first
    for u in range(2 * end, count - lo):
        written(u)


def build(nc, x, src, dst, edge_attr, WQ, WK, WE, WV, WO, bO, ln1_g, ln1_b, W1, b1, W2, b2, ln2_g, ln2_b,
          qk_w, qk_b, v_w, v_b, o_w, o_b, ln_g, ln_b, out):
    f32, i32 = mybir.dt.float32, mybir.dt.int32
    ALU, ACT, AX = mybir.AluOpType, mybir.ActivationFunctionType, mybir.AxisListType
    ctx = ExitStack()
    with ctx:
        ctx.enter_context(nc.allow_non_contiguous_dma(reason="columns of biases, and single edges"))

        def sb(name, shape, dt=f32):
            return ctx.enter_context(nc.sbuf_tensor(name, shape, dt))

        def pb(name, shape):
            return ctx.enter_context(nc.psum_tensor(name, shape, f32))

        def sem(name):
            return ctx.enter_context(nc.semaphore(name))

        def dram(name, shape):
            return nc.dram_tensor(name, shape, f32)

        normed1 = dram("normed1", [N, D])
        x1 = dram("x1", [N, D])
        ends = [dram(f"ends{l}", [EUNITS, 128, 2 * GP, D]) for l in range(3)]
        targets = [dram(f"targets{l}", [EUNITS, 128, GP, D]) for l in range(3)]
        sums = [dram(f"sums{l}", [EUNITS, 128, GP, PW]) for l in range(3)]
        table = [x, normed1, x1]
        result = [normed1, x1, out]

        ident = sb("ident", [128, 128])
        center = sb("center", [128, 128])
        mean = sb("mean", [128, 128])
        center_in = sb("center_in", [128, 128])
        center_1 = [sb(f"center_1{l}", [128, 128]) for l in range(2)]
        first_row = sb("first_row", [128, 128])
        bias_kv = sb("bias_kv", [128, 4, 128])
        bias_q = sb("bias_q", [128, 8, 64])
        w_kv = [sb(f"w_kv{l}", [128, 128]) for l in range(3)]
        w_q = [sb(f"w_q{l}", [128, 128]) for l in range(3)]
        w_e = [sb(f"w_e{l}", [128, 128]) for l in range(2)]
        w_o = [sb(f"w_o{l}", [128, 128]) for l in range(3)]
        w_1 = [sb(f"w_1{l}", [128, 128]) for l in range(2)]
        w_2 = [sb(f"w_2{l}", [128, 64]) for l in range(2)]
        wtmp = sb("wtmp", [64, 3, 128])
        wsum = sb("wsum", [128, 8])
        vec = sb("vec", [128, 32])
        names = {}

        CENTRED = {"bO0": "cb0", "in1": "cb1", "ob": "cb2", "obf": "cbf", "y0": "zb0", "y1": "zb1"}

        def col(name):
            k = names.setdefault(name, len(names))
            return vec[:, k:k + 1]

        eps_col = col("eps")

        src_i = sb("src_i", [128, ET], i32)
        dst_i = sb("dst_i", [128, ET], i32)
        prev_i = sb("prev_i", [128, 1], i32)
        next_i = sb("next_i", [128, 1], i32)
        dst_f = sb("dst_f", [128, ET])
        shift_f = sb("shift_f", [128, ET])
        far_f = sb("far_f", [128, ET])
        zero_f = sb("zero_f", [128, ET])
        cont = sb("cont", [128, ET])
        head = sb("head", [128, ET])
        gidx = sb("gidx", [128, EUNITS, 2 * GP], i32)
        sidx = sb("sidx", [128, ET], i32)
        through = sb("through", [128, PW])
        throughT = sb("throughT", [PW, 128])
        carryT = sb("carryT", [PW, 136])
        carry = sb("carry", [128, PW])

        X = sb("X", [128, 2, 2 * GP, D])
        XM = sb("XM", [128, 2, 2 * GP, D])
        SQ0 = sb("SQ0", [128, 2, 2 * GP, D])
        N0 = sb("N0", [128, 2, 2 * GP, D])
        HT = sb("HT", [128, 2, 2, 4, 128])
        SQ1 = sb("SQ1", [128, 2, 512])
        LG1 = sb("LG1", [128, 512])
        R1 = sb("R1", [128, 2, 512])
        NT = sb("NT", [128, 2, 512])
        HID = sb("HID", [128, 2, 512])
        ZT = sb("ZT", [128, 2, 4, 128])
        SQ2 = sb("SQ2", [128, 2, GP, D])
        N2 = sb("N2", [128, 2, GP, D])
        NG = sb("NG", [128, GP, D])
        XS = sb("XS", [128, GP, D])
        gain_row = sb("gain_row", [128, D])
        shift_row = sb("shift_row", [128, D])
        OUT = sb("OUT", [128, 2, GP, D])
        X2 = sb("X2", [128, 2, GP, D])
        EA = sb("EA", [128, 2, GP, D])
        EAT = sb("EAT", [128, 4, 128])
        QS = sb("QS", [128, GP, D])
        PR = sb("PR", [128, GP, D])
        PR2 = sb("PR2", [128, GP, D])
        SC = sb("SC", [128, 2, GP * 4])
        PAY = sb("PAY", [128, 2, GP, PW])
        S = sb("S", [128, 2, GP, PW])
        SIN = sb("SIN", [128, 2, GP, PW])
        T = sb("T", [128, 2, GP, PW])
        ZR = sb("ZR", [128, 2, 2, GP * 4])
        ATT = sb("ATT", [128, 2, GP, D])
        ATTT = sb("ATTT", [128, 2, 4, 128])
        CB = sb("CB", [128, 2, GP])
        st0 = sb("st0", [128, 2, 4, 2 * GP])
        st2 = sb("st2", [128, 2, 4, GP])
        GB = sb("GB", [128, 2, 2 * GP, D])
        IB = sb("IB", [128, 2, 2 * GP], i32)

        banks = pb("banks", [128, 8, 512])
        psT = [banks[:, h, :] for h in range(2)]
        psC = [banks[:, 2 + h, :] for h in range(2)]
        psH = [banks[:, 4 + q, :] for q in range(2)]
        psZ, psN = banks[:, 6, :], banks[:, 7, :]
        psX = [banks[:, k, :] for k in range(3)]
        psKV = banks[:, 3:5, :].rearrange("p q (j c) -> p j q c", c=128)
        psQ, psE = banks[:, 5, :], banks[:, 6, :]

        def rows8(ap):
            return ap.rearrange("p (g d) -> p g d", d=D)

        DENSE = [("dense", l) for l in range(3)]
        EDGE = [("edge", l) for l in range(3)]
        FIX = [("fix", l) for l in range(3)]
        UPD = DENSE + FIX
        FFN = [p for p in UPD if p[1] < 2]
        BACK = [p for p in UPD if p[1] > 0]
        P1 = [p for p in UPD if p[1] == 1]
        owner = {"dve": [], "act": [], "pe": []}

        def count(eng, name, phases):
            c = Count(sem(name), phases)
            owner[eng].append(c)
            return c

        xsum = count("dve", "xsum", RAW)
        xm = count("dve", "xm", RAW)
        sq0 = count("act", "sq0", RAW)
        ss0 = count("dve", "ss0", RAW)
        lg0 = count("act", "lg0", RAW)
        r0 = count("act", "r0", RAW)
        n0 = count("dve", "n0", RAW)
        tp1 = count("pe", "tp1", UPD)
        ht = count("dve", "ht", UPD)
        c1 = count("pe", "c1", UPD)
        sq1 = count("act", "sq1", UPD)
        var1 = count("pe", "var1", UPD)
        lg1 = count("act", "lg1", UPD)
        r1 = count("act", "r1", UPD)
        n1 = count("dve", "n1", UPD)
        h1 = [count("pe", f"h1{q}", FFN) for q in range(2)]
        hid = count("act", "hid", FFN)
        c2 = count("pe", "c2", FFN)
        zt = count("act", "zt", UPD)
        tz = count("pe", "tz", UPD)
        sq2 = count("act", "sq2", FFN)
        ss2 = count("dve", "ss2", FFN)
        lg2 = count("act", "lg2", FFN)
        r2 = count("act", "r2", FFN)
        n2 = count("dve", "n2", FFN)
        ng = count("dve", "ng", P1)
        xs = count("dve", "xs", P1)
        res = count("dve", "res", BACK)
        fb = count("dve", "fb", FIX)
        ts = count("dve", "ts", FIX)
        ze = count("dve", "ze", FIX)
        zr = count("dve", "zr", FIX)
        att = count("dve", "att", FIX)
        tpa = count("pe", "tpa", FIX)
        attT = count("act", "attT", FIX)
        tpe = count("pe", "tpe", EDGE)
        hs = count("act", "hs", EDGE)
        hd = count("act", "hd", EDGE)
        ea = count("act", "ea", EDGE[:2])
        pq = count("pe", "pq", EDGE)
        pkv = count("pe", "pkv", EDGE)
        qs = count("act", "qs", EDGE)
        pr = count("dve", "pr", EDGE)
        pr2 = count("dve", "pr2", EDGE[:2])
        sc = count("dve", "sc", EDGE)
        cl = count("dve", "cl", EDGE)
        cl2 = count("dve", "cl2", EDGE)
        ex = count("act", "ex", EDGE)
        pv = count("dve", "pv", EDGE)
        cb = count("dve", "cb", EDGE)
        sw = count("dve", "sw", EDGE)

        def slots(name, phases):
            return Slots([sem(f"{name}{h}") for h in range(2)], phases)

        ld_x = slots("ld_x", RAW)
        ld_n = slots("ld_n", [p for p in PHASES if p not in RAW])
        ld_r = slots("ld_r", BACK)
        ld_ea = slots("ld_ea", EDGE[:2])
        ld_s = slots("ld_s", FIX)
        st_out = slots("st_out", DENSE)
        st_n = slots("st_n", [EDGE[0], EDGE[2]])
        st_s = slots("st_s", EDGE)
        sc_out = slots("sc_out", FIX)
        sweep = sem("sweep")
        gathered = [sem(f"gathered{h}") for h in range(2)]
        ends_out = [sem(f"ends_out{h}") for h in range(2)]
        idx_copied = sem("idx_copied")
        phase_end = sem("phase_end")
        w_loaded, w_ready, ones_set, prep = sem("w_loaded"), sem("w_ready"), sem("ones_set"), sem("prep")
        pool_set, passed = sem("pool_set"), sem("passed")
        w_turned, w_taken = sem("w_turned"), sem("w_taken")
        e_loaded, idx_ready = sem("e_loaded"), sem("idx_ready")
        c_turn, c_scan, c_back, c_ready = sem("c_turn"), sem("c_scan"), sem("c_back"), sem("c_ready")

        def shift1(ph):
            return col("cbf") if ph == ("fix", 2) else col(f"cb{ph[1]}")

        def last(ph):
            return res if ph in BACK else n2

        def leaving(ph):
            return OUT if ph in BACK else N2

        def barrier(eng, ph):
            eng.drain().then_inc(phase_end, 1)
            eng.wait_ge(phase_end, 5 * (PHASES.index(ph) + 1))

        wide = {ph: (2 if ph[0] == "edge" else 1) * GP for ph in PHASES}

        def w(eng, what):
            eng.wait_ge(*what)

        vectors = []
        for l in range(2):
            vectors += [(f"bO{l}", bO[l]), (f"g1{l}", ln1_g[l]), (f"s1{l}", ln1_b[l]), (f"b2{l}", b2[l]),
                        (f"g2{l}", ln2_g[l]), (f"s2{l}", ln2_b[l])]
        vectors += [("ob", o_b), ("vb", v_b), ("lg", ln_g), ("ls", ln_b)]
        for name, _ in vectors:
            col(name)
        for l in range(2):
            col(f"fb{l}")
            col(f"y{l}")
            col(f"zb{l}")
        for name in ("in1", "obf", "cb0", "cb1", "cb2", "cbf"):
            col(name)
        N_W = 2 * len(vectors) + 2 + 2 * (2 * 4 + 2 + 2 + 1) + 2 * 3 + 4 + 8 + 2

        block = ctx.enter_context(nc.Block())

        @block.sync
        def _(sp):
            sp.wait_ge(ones_set, 1)
            sp.dma_start(src_i[0:EP, :], src.rearrange("(p t) -> p t", t=ET)).then_inc(e_loaded, 16)
            sp.dma_start(dst_i[0:EP, :], dst.rearrange("(p t) -> p t", t=ET)).then_inc(e_loaded, 16)
            grid = dst.rearrange("(p t) -> p t", t=ET)
            sp.dma_start(prev_i[1:EP, :], grid[0:EP - 1, ET - 1:ET]).then_inc(e_loaded, 16)
            sp.dma_start(next_i[0:EP - 1, :], grid[1:EP, 0:1]).then_inc(e_loaded, 16)
            n_w = 0

            def load(to, what):
                nonlocal n_w
                n_w += 1
                sp.dma_start(to, what).then_inc(w_loaded, 16)

            for name, v in vectors:
                for q in range(2):
                    load(col(name)[64 * q:64 * q + 64, :], v.rearrange("(p a) -> p a", a=1))
            for l in range(2):
                load(col(f"fb{l}"), b1[l].rearrange("(p a) -> p a", a=1))
                for q in range(2):
                    p = slice(64 * q, 64 * q + 64)
                    load(w_kv[l][p, 0:64], WK[l])
                    load(w_kv[l][p, 64:128], WV[l])
                    load(w_q[l][p, p], WQ[l])
                    load(w_e[l][p, p], WE[l])
                    load(w_o[l][p, p], WO[l])
                    load(w_1[l][p, :], W1[l])
                load(w_2[l][:, :], W2[l])
            for k, m in enumerate((qk_w, v_w, o_w)):
                for q in range(2):
                    load(wtmp[:, k, 64 * q:64 * q + 64], m)
            for j in range(4):
                load(bias_kv[0:1, j, 0:64], qk_b.rearrange("(a n) -> a n", a=1))
            for g in range(8):
                load(bias_q[0:1, g, :], qk_b.rearrange("(a n) -> a n", a=1))
            load(gain_row[:, :], ln2_g[1:2, :].to_broadcast([128, D]))
            load(shift_row[:, :], ln2_b[1:2, :].to_broadcast([128, D]))
            assert n_w == N_W, (n_w, N_W)

            def node_rows(t, n, parts=slice(0, 128)):
                m = parts.stop - parts.start
                return t[bass.ds(n * ROWS + parts.start * GP, m * GP), :].rearrange("(p g) d -> p g d", g=GP)

            def part(ph, u):
                return slice(0, TAIL if ph[0] == "dense" and isinstance(u.n, int) and u.n == UNITS - 1 else 128)

            def load_x(ph, u):
                p, h = part(ph, u), u.slot
                w(sp, xm.before(ph, u))
                if ph[0] == "dense":
                    sp.dma_start(X[p, h, 0:GP, :], node_rows(table[ph[1]], u.n, p)).then_inc(ld_x.sems[h], 16)
                else:
                    sp.dma_start(X[:, h, :, :], ends[ph[1]][u.n, :, :, :]).then_inc(ld_x.sems[h], 16)

            def load_n(ph, u):
                p, h = part(ph, u), u.slot
                w(sp, (tpe if ph[0] == "edge" else tp1).before(ph, u))
                if ph[0] == "dense":
                    sp.dma_start(N0[p, h, 0:GP, :], node_rows(normed1, u.n, p)).then_inc(ld_n.sems[h], 16)
                elif ph[0] == "edge":
                    sp.dma_start(N0[:, h, :, :], ends[1][u.n, :, :, :]).then_inc(ld_n.sems[h], 16)
                elif ph[1] == 1:
                    sp.dma_start(N0[:, h, 0:GP, :], ends[1][u.n, :, GP:2 * GP, :]).then_inc(ld_n.sems[h], 16)
                else:
                    sp.dma_start(N0[:, h, 0:GP, :], targets[ph[1]][u.n, :, :, :]).then_inc(ld_n.sems[h], 16)

            def load_r(ph, u):
                p, h = part(ph, u), u.slot
                w(sp, res.before(ph, u))
                if ph[0] == "dense":
                    sp.dma_start(X2[p, h, :, :], node_rows(x if ph[1] == 1 else x1, u.n, p)).then_inc(ld_r.sems[h], 16)
                else:
                    sp.dma_start(X2[:, h, :, :], ends[0 if ph[1] == 1 else 2][u.n, :, GP:2 * GP, :]).then_inc(ld_r.sems[h], 16)

            def load_ea(ph, u):
                w(sp, tpe.before(ph, u))
                e3 = edge_attr.rearrange("(p t) d -> p t d", t=ET)
                sp.dma_start(EA[0:EP, u.slot, :, :], e3[:, bass.ds(u.n * GP, GP), :]).then_inc(ld_ea.sems[u.slot], 16)

            def load_s(ph, u):
                w(sp, ts.before(ph, u))
                sp.dma_start(SIN[:, u.slot, :, :], sums[ph[1]][u.n, :, :, :]).then_inc(ld_s.sems[u.slot], 16)

            def store_rows(ph, u):
                p, h = part(ph, u), u.slot
                w(sp, last(ph).done(ph, u))
                sp.dma_start(node_rows(result[ph[1]], u.n, p), leaving(ph)[p, h, :, :]).then_inc(st_out.sems[h], 16)

            def store_sums(ph, u):
                w(sp, sw.done(ph, u))
                sp.dma_start(sums[ph[1]][u.n, :, :, :], S[:, u.slot, :, :]).then_inc(st_s.sems[u.slot], 16)

            def store_targets(ph, u):
                w(sp, n0.done(ph, u))
                sp.dma_start(targets[ph[1]][u.n, :, :, :], N0[:, u.slot, GP:2 * GP, :]).then_inc(st_n.sems[u.slot], 16)

            def update(ph):
                end = -1 if ph in FFN else 0

                def body(at):
                    if ph in RAW:
                        for u in at(5):
                            load_x(ph, u)
                    else:
                        for u in at(4):
                            load_n(ph, u)
                    if ph in FIX:
                        for u in at(5):
                            load_s(ph, u)
                    if ph in DENSE:
                        for u in at(end):
                            store_rows(ph, u)
                    if ph in BACK:
                        for u in at(end + 2):
                            load_r(ph, u)
                return body

            def edges(ph):
                def body(at):
                    if ph in RAW:
                        for u in at(3):
                            load_x(ph, u)
                        for u in at(1):
                            store_targets(ph, u)
                    for u in at(2):
                        if ph not in RAW:
                            load_n(ph, u)
                        if ph[1] < 2:
                            load_ea(ph, u)
                    for u in at(0):
                        store_sums(ph, u)
                return body

            def run(ph):
                u = units(ph)
                if ph[0] == "edge":
                    periods(sp, u, 0, 3, edges(ph))
                else:
                    periods(sp, u, -1, 6, update(ph))
                for slot, phases in ((st_out, DENSE), (st_n, [EDGE[0], EDGE[2]]), (st_s, EDGE)):
                    if ph in phases:
                        for h in range(2):
                            w(sp, slot.done(ph, Unit((u + 1 - h) // 2 - 1, h)))
                barrier(sp, ph)

            sp.wait_ge(prep, 4)
            for ph in PHASES:
                run(ph)

        @block.gpsimd
        def _(pool):
            pool.memset(ident[:, :], 0.0).then_inc(pool_set, 1)
            pool.wait_ge(pool_set, 1)
            pool.affine_select(out=ident[:, :], in_=ident[:, :], compare_op=ALU.not_equal, fill=1.0,
                               base=0, pattern=[[-1, 128]], channel_multiplier=1).then_inc(pool_set, 1)
            pool.wait_ge(idx_ready, 1)
            pool.drain().then_inc(prep, 1)

            def hold(sem_, value):
                pool.wait_ge(sem_, value)
                pool.sem_inc(passed, 1)

            def gather(l):
                before = l * EUNITS

                def fetch(u, h, k):
                    if l or not (isinstance(k, int) and k == 0):
                        hold(ends_out[h], 16 * (k + l * ((EUNITS + 1 - h) // 2)))
                    pool.tensor_copy(IB[:, h, :], gidx[:, bass.ds(u, 1), :].rearrange("p a k -> p (a k)")).then_inc(idx_copied, 1)
                    hold(idx_copied, idx_base[0] + u + 1)
                    for g in range(2 * GP):
                        pool.indirect_dma_start(out=GB[:, h, g, :], out_offset=None, in_=table[l][:, :],
                                                in_offset=bass.IndirectOffsetOnAxis(ap=IB[:, h, g:g + 1], axis=0)
                                                ).then_inc(gathered[h], 16)

                def put(u, h, k):
                    hold(gathered[h], 16 * 2 * GP * (k + 1 + l * ((EUNITS + 1 - h) // 2)))
                    pool.dma_start(ends[l][u, :, :, :], GB[:, h, :, :]).then_inc(ends_out[h], 16)

                fetch(0, 0, 0)
                with pool.Fori(0, EUNITS // 2) as i:
                    fetch(2 * i + 1, 1, i)
                    put(2 * i, 0, i)
                    fetch(2 * i + 2, 0, i + 1)
                    put(2 * i + 1, 1, i)
                put(EUNITS - 1, 0, EUNITS // 2)
                idx_base[0] += EUNITS
                for h in range(2):
                    pool.wait_ge(ends_out[h], 16 * (l + 1) * ((EUNITS + 1 - h) // 2))

            idx_base = [0]

            def scatter(ph):
                def one(i, h):
                    n, u = 2 * i + h, Unit(i, h)
                    hold(sc_out.sems[h], GP * sc_out.base[ph][h] + 16 * GP * i)
                    pool.tensor_copy(IB[:, h, 0:GP], sidx[:, bass.ds(n * GP, GP)]).then_inc(idx_copied, 1)
                    hold(idx_copied, idx_base[0] + n + 1)
                    hold(*last(ph).done(ph, u))
                    for g in range(GP):
                        pool.indirect_dma_start(out=result[ph[1]][:, :],
                                                out_offset=bass.IndirectOffsetOnAxis(ap=IB[:, h, g:g + 1], axis=0),
                                                in_=leaving(ph)[:, h, g, :], in_offset=None,
                                                bounds_check=N - 1, oob_is_err=False).then_inc(sc_out.sems[h], 16)

                with pool.Fori(0, EUNITS // 2) as i:
                    one(i, 0)
                    one(i, 1)
                one(EUNITS // 2, 0)
                idx_base[0] += EUNITS
                for h in range(2):
                    pool.wait_ge(sc_out.sems[h], GP * (sc_out.base[ph][h] + 16 * ((EUNITS + 1 - h) // 2)))

            pool.wait_ge(prep, 4)
            for ph in PHASES:
                if ph[0] == "dense":
                    gather(ph[1])
                if ph[0] == "fix":
                    scatter(ph)
                barrier(pool, ph)

        @block.scalar
        def _(act):
            act.add_instruction(mybir.InstLoadActFuncSet(name=nc.get_next_instruction_name(), act_func_set_id=LN_EXP_SET, engine=mybir.EngineType.Activation))
            for c in owner["act"]:
                act.sem_inc(c.sem, 2)
            act.drain().then_inc(prep, 1)
            act.wait_ge(prep, 4)

            def square0(ph, u):
                g = wide[ph]
                w(act, xm.done(ph, u))
                act.activation(SQ0[:, u.slot, 0:g, :], XM[:, u.slot, 0:g, :], ACT.Square).then_inc(sq0.sem, 1)

            def rstd(ph, u, st, g, ss, lg, r):
                h = u.slot
                w(act, ss.done(ph, u))
                act.activation(st[:, h, 2, 0:g], st[:, h, 1, 0:g], ACT.Ln, bias=eps_col, scale=1.0 / D).then_inc(lg.sem, 1)
                w(act, lg.done(ph, u))
                act.activation(st[:, h, 3, 0:g], st[:, h, 2, 0:g], ACT.Exp, scale=-0.5).then_inc(r.sem, 1)

            def square1(ph, u):
                w(act, c1.done(ph, u))
                act.activation(SQ1[:, u.slot, :], psC[u.slot], ACT.Square, bias=shift1(ph)).then_inc(sq1.sem, 1)

            def rstd1(ph, u):
                w(act, var1.done(ph, u))
                act.activation(LG1[:, :], psT[u.slot], ACT.Ln, bias=eps_col).then_inc(lg1.sem, 1)
                w(act, lg1.done(ph, u))
                act.activation(R1[:, u.slot, :], LG1[:, :], ACT.Exp, scale=-0.5).then_inc(r1.sem, 1)

            def hidden(ph, u):
                for q in range(2):
                    w(act, h1[q].done(ph, u))
                    ins = act.activation(HID[:, q, :], psH[q], ACT.Relu, bias=col(f"fb{ph[1]}"), scale=1.0)
                ins.then_inc(hid.sem, 1)

            def turned_out(ph, u):
                h = u.slot
                to = ZT[:, h, :, :].rearrange("p j n -> p (j n)")
                if ph in FFN:
                    w(act, c2.done(ph, u))
                    ins = act.activation(to, psZ, ACT.Identity, bias=col(f"zb{ph[1]}"), scale=1.0)
                else:
                    w(act, n1.done(ph, u))
                    w(act, tz.before(ph, u))
                    ins = act.activation(to, NT[:, h, :], ACT.Identity, bias=col("ls"), scale=col("lg"))
                ins.then_inc(zt.sem, 1)

            def square2(ph, u):
                w(act, tz.done(ph, u))
                act.activation(SQ2[:, u.slot, :, :], rows8(psN), ACT.Square).then_inc(sq2.sem, 1)

            def att_turned(ph, u):
                w(act, tpa.done(ph, u))
                act.activation(ATTT[:, u.slot, :, :].rearrange("p j n -> p (j n)"), psC[u.slot], ACT.Copy).then_inc(attT.sem, 1)

            def update(ph):
                end = -1 if ph in FFN else 0

                def body(at):
                    for u in at(end):
                        turned_out(ph, u)
                    for u in at(1):
                        square1(ph, u)
                    if ph in FFN:
                        for u in at(-1):
                            square2(ph, u)
                    if ph in RAW:
                        for u in at(2):
                            rstd(ph, u, st0, GP, ss0, lg0, r0)
                    if ph in FFN:
                        for u in at(0):
                            hidden(ph, u)
                        for u in at(-1):
                            rstd(ph, u, st2, GP, ss2, lg2, r2)
                    for u in at(1):
                        rstd1(ph, u)
                    if ph in FIX:
                        for u in at(2):
                            att_turned(ph, u)
                    if ph in RAW:
                        for u in at(3):
                            square0(ph, u)
                return body

            def edges(ph):
                l = ph[1]
                hh = HEADS[l]

                def one(u):
                    w(act, tpe.done(ph, u))
                    for k, s_ in ((0, hs), (1, hd)):
                        w(act, (pkv if k == 0 else pq).before(ph, u, 1))
                        to = HT[:, 0, k, :, :].rearrange("p j n -> p (j n)")
                        if l == 1:
                            act.activation(to, psX[k], ACT.Identity, bias=col("s20"), scale=col("g20")).then_inc(s_.sem, 1)
                        else:
                            act.activation(to, psX[k], ACT.Copy).then_inc(s_.sem, 1)
                    if l < 2:
                        act.activation(EAT[:, :, :].rearrange("p j n -> p (j n)"), psX[2], ACT.Copy).then_inc(ea.sem, 1)
                    w(act, pq.done(ph, u))
                    w(act, pr.before(ph, u, 1))
                    act.activation(QS[:, :, :], rows8(psQ), ACT.Copy).then_inc(qs.sem, 1)
                    w(act, cl2.done(ph, u))
                    w(act, sw.before(ph, u))
                    act.activation(PAY[:, u.slot, :, D:D + hh], SC[:, 1, 0:GP * hh].rearrange("p (g k) -> p g k", k=hh),
                                   ACT.Exp).then_inc(ex.sem, 1)

                def body(at):
                    if ph in RAW:
                        for u in at(1):
                            square0(ph, u)
                    for u in at(0):
                        one(u)
                    if ph in RAW:
                        for u in at(1):
                            rstd(ph, u, st0, 2 * GP, ss0, lg0, r0)
                return body

            for ph in PHASES:
                if ph[0] == "edge":
                    periods(act, units(ph), 0, 1, edges(ph))
                else:
                    periods(act, units(ph), -1, 3, update(ph))
                barrier(act, ph)

        @block.vector
        def _(dve):
            for c in owner["dve"]:
                dve.sem_inc(c.sem, 2)
            done = [0]

            def step(ins):
                done[0] += 1
                ins.then_inc(ones_set, 1)
                return done[0]

            def chain(ins):
                step(ins)
                dve.wait_ge(ones_set, done[0])

            for t in (dst_i, src_i):
                dve.memset(t[:, :], FAR if t is dst_i else 0)
            dve.memset(prev_i[:, :], -1)
            dve.memset(next_i[:, :], -1)
            for t in (EA, S, X, N0, X2):
                dve.memset(t[:, :, :, :], 0.0)
            for t in (first_row, vec, *w_q, *w_e, *w_o):
                dve.memset(t[:, :], 0.0)
            dve.memset(bias_kv[:, :, :], 0.0)
            dve.memset(bias_q[:, :, :], 0.0)
            dve.memset(zero_f[:, :], 0.0)
            dve.memset(carryT[:, :], 0.0)
            dve.memset(PAY[:, :, :, :], 0.0)
            chain(dve.drain())
            dve.memset(first_row[0:1, :], 1.0)
            dve.memset(eps_col, EPS)
            dve.memset(center[:, :], 0.0)
            chain(dve.drain())
            dve.memset(center[0:64, 0:64], -1.0 / D)
            dve.memset(center[64:128, 64:128], -1.0 / D)
            dve.wait_ge(pool_set, 2)
            chain(dve.drain())
            dve.tensor_scalar(out=mean[:, :], in0=center[:, :], scalar1=-1.0, scalar2=None, op0=ALU.mult)
            chain(dve.drain())
            chain(dve.tensor_tensor(out=center[:, :], in0=center[:, :], in1=ident[:, :], op=ALU.add))
            dve.wait_ge(e_loaded, 64)
            chain(dve.tensor_copy(dst_f[:, :], dst_i[:, :]))
            dve.tensor_copy(shift_f[:, 1:ET], dst_f[:, 0:ET - 1])
            dve.tensor_copy(shift_f[:, 0:1], prev_i[:, :])
            chain(dve.drain())
            chain(dve.tensor_tensor(out=cont[:, :], in0=dst_f[:, :], in1=shift_f[:, :], op=ALU.is_equal))
            chain(dve.tensor_tensor_scan(out=head[:, :], data0=cont[:, :], data1=zero_f[:, :], initial=1.0,
                                         op0=ALU.mult, op1=ALU.add))
            dve.tensor_copy(through[:, :], head[:, ET - 1:ET].to_broadcast([128, PW]))
            dve.memset(cont[:, 0:1], 0.0)
            dve.tensor_copy(shift_f[:, 0:ET - 1], dst_f[:, 1:ET])
            dve.tensor_copy(shift_f[:, ET - 1:ET], next_i[:, :])
            chain(dve.drain())
            chain(dve.tensor_tensor(out=far_f[:, :], in0=dst_f[:, :], in1=shift_f[:, :], op=ALU.is_equal))
            chain(dve.scalar_tensor_tensor(out=far_f[:, :], in0=far_f[:, :], scalar=float(FAR), in1=dst_f[:, :],
                                           op0=ALU.mult, op1=ALU.add))
            dve.tensor_copy(sidx[:, :], far_f[:, :])
            dve.tensor_copy(gidx[:, :, 0:GP], src_i[:, :].rearrange("p (u g) -> p u g", g=GP))
            chain(dve.tensor_scalar(out=dst_f[:, :], in0=dst_f[:, :], scalar1=float(N - 1), scalar2=None, op0=ALU.min))
            dve.tensor_copy(gidx[:, :, GP:2 * GP], dst_f[:, :].rearrange("p (u g) -> p u g", g=GP))
            dve.drain().then_inc(idx_ready, 1)
            dve.wait_ge(w_loaded, 16 * N_W)
            dve.wait_ge(w_turned, 3)
            for q in range(2):
                p = slice(64 * q, 64 * q + 64)
                dve.tensor_copy(w_kv[2][p, 0:64], banks[p, 0, 0:64])
                dve.tensor_copy(w_kv[2][p, 64:128], banks[p, 1, 0:64])
                dve.tensor_copy(w_q[2][p, p], banks[p, 0, 0:64])
                dve.tensor_copy(w_o[2][p, p], banks[p, 2, 0:64])
            dve.drain().then_inc(w_taken, 1)
            for l in range(2):
                dve.tensor_tensor(out=col(f"y{l}"), in0=col(f"s1{l}"), in1=col(f"b2{l}"), op=ALU.add)
                dve.tensor_scalar(out=center_1[l][:, :], in0=center[:, :], scalar1=col(f"g1{l}"), scalar2=None, op0=ALU.mult)
            dve.tensor_scalar(out=center_in[:, :], in0=center[:, :], scalar1=col("g20"), scalar2=None, op0=ALU.mult)
            dve.tensor_tensor(out=col("in1"), in0=col("s20"), in1=col("bO1"), op=ALU.add)
            dve.wait_ge(w_turned, 6)
            for l in range(2):
                dve.tensor_tensor(out=col(f"fb{l}"), in0=col(f"fb{l}"), in1=banks[:, 4 + l, 0:1], op=ALU.add)
            dve.tensor_tensor(out=col("obf"), in0=col("ob"), in1=banks[:, 6, 0:1], op=ALU.add)
            dve.tensor_copy(throughT[:, :], banks[0:PW, 7, 0:128])
            for l in range(2):
                dve.tensor_scalar(out=w_1[l][:, :], in0=w_1[l][:, :], scalar1=col(f"g1{l}"), scalar2=None, op0=ALU.mult)
            dve.drain().then_inc(w_taken, 1)
            dve.wait_ge(w_turned, 7)
            for k, name in enumerate(CENTRED):
                dve.tensor_copy(col(CENTRED[name]), banks[:, 0, k:k + 1])
            for l in range(3):
                for q in range(2):
                    p = slice(64 * q, 64 * q + 64)
                    dve.tensor_reduce(out=wsum[p, l:l + 1], in_=w_o[l][p, p], axis=AX.X, op=ALU.add)
            for l in range(2):
                dve.tensor_reduce(out=wsum[:, 3 + l:4 + l], in_=w_2[l][:, :], axis=AX.X, op=ALU.add)
            chain(dve.drain())
            chain(dve.tensor_scalar(out=wsum[:, 0:5], in0=wsum[:, 0:5], scalar1=1.0 / D, scalar2=None, op0=ALU.mult))
            for l in range(3):
                for q in range(2):
                    p = slice(64 * q, 64 * q + 64)
                    dve.tensor_scalar(out=w_o[l][p, p], in0=w_o[l][p, p], scalar1=wsum[p, l:l + 1], scalar2=None,
                                      op0=ALU.subtract)
            for l in range(2):
                dve.tensor_scalar(out=w_2[l][:, :], in0=w_2[l][:, :], scalar1=wsum[:, 3 + l:4 + l], scalar2=None,
                                  op0=ALU.subtract)
            dve.drain().then_inc(prep, 1)
            dve.wait_ge(prep, 4)

            def front_a(ph, u):
                g, h = wide[ph], u.slot
                w(dve, ld_x.done(ph, u))
                dve.tensor_reduce(out=st0[:, h, 0, 0:g], in_=X[:, h, 0:g, :], axis=AX.X, op=ALU.add).then_inc(xsum.sem, 1)
                w(dve, xsum.done(ph, u))
                dve.scalar_tensor_tensor(out=XM[:, h, 0:g, :], in0=st0[:, h, 0, 0:g].unsqueeze(2).to_broadcast([128, g, D]),
                                         scalar=-1.0 / D, in1=X[:, h, 0:g, :], op0=ALU.mult, op1=ALU.add
                                         ).then_inc(xm.sem, 1)

            def squares0(ph, u):
                g, h = wide[ph], u.slot
                w(dve, sq0.done(ph, u))
                dve.tensor_reduce(out=st0[:, h, 1, 0:g], in_=SQ0[:, h, 0:g, :], axis=AX.X, op=ALU.add).then_inc(ss0.sem, 1)

            def norm_x(ph, u):
                g, h = wide[ph], u.slot
                w(dve, r0.done(ph, u))
                w(dve, (tpe if ph[0] == "edge" else tp1).before(ph, u))
                if ph[0] == "edge":
                    w(dve, st_n.before(ph, u))
                dve.scalar_tensor_tensor(out=N0[:, h, 0:g, :], in0=XM[:, h, 0:g, :], scalar=0.0,
                                         in1=st0[:, h, 3, 0:g].unsqueeze(2).to_broadcast([128, g, D]),
                                         op0=ALU.max, op1=ALU.mult).then_inc(n0.sem, 1)

            def h_turned(ph, u):
                w(dve, tp1.done(ph, u))
                dve.tensor_copy(HT[:, u.slot, 0, :, :].rearrange("p j n -> p (j n)"), psT[u.slot]).then_inc(ht.sem, 1)

            def norm1(ph, u):
                h = u.slot
                w(dve, r1.done(ph, u))
                if ph not in FFN:
                    w(dve, zt.before(ph, u))
                dve.scalar_tensor_tensor(out=NT[:, h, :], in0=psC[h], scalar=shift1(ph), in1=R1[:, h, :],
                                         op0=ALU.add, op1=ALU.mult).then_inc(n1.sem, 1)

            def free_out(ph, u):
                if ph[0] == "dense":
                    w(dve, st_out.before(ph, u))
                else:
                    dve.wait_ge(sc_out.sems[u.slot], GP * sc_out.base[ph][u.slot] + 16 * GP * u.turn)

            def squares2(ph, u):
                w(dve, sq2.done(ph, u))
                dve.tensor_reduce(out=st2[:, u.slot, 1, :], in_=SQ2[:, u.slot, :, :], axis=AX.X, op=ALU.add).then_inc(ss2.sem, 1)

            def norm2(ph, u):
                h = u.slot
                w(dve, r2.done(ph, u))
                if ph not in BACK:
                    free_out(ph, u)
                dve.tensor_tensor(out=N2[:, h, :, :], in0=rows8(psN),
                                  in1=st2[:, h, 3, :].unsqueeze(2).to_broadcast([128, GP, D]), op=ALU.mult
                                  ).then_inc(n2.sem, 1)

            def residual(ph, u):
                h = u.slot
                w(dve, ld_r.done(ph, u))
                if ph in P1:
                    w(dve, n2.done(ph, u))
                    dve.tensor_tensor(out=NG[:, :, :], in0=N2[:, h, :, :],
                                      in1=gain_row[:, :].unsqueeze(1).to_broadcast([128, GP, D]), op=ALU.mult).then_inc(ng.sem, 1)
                    dve.tensor_tensor(out=XS[:, :, :], in0=X2[:, h, :, :],
                                      in1=shift_row[:, :].unsqueeze(1).to_broadcast([128, GP, D]), op=ALU.add).then_inc(xs.sem, 1)
                    w(dve, xs.done(ph, u))
                    free_out(ph, u)
                    ins = dve.tensor_tensor(out=OUT[:, h, :, :], in0=NG[:, :, :], in1=XS[:, :, :], op=ALU.add)
                else:
                    w(dve, tz.done(ph, u))
                    free_out(ph, u)
                    ins = dve.tensor_tensor(out=OUT[:, h, :, :], in0=rows8(psN), in1=X2[:, h, :, :], op=ALU.add)
                ins.then_inc(res.sem, 1)

            def attention(ph, u):
                h, hh = u.slot, HEADS[ph[1]]
                dve.tensor_copy(CB[:, h, :], head[:, bass.ds(u.n * GP, GP)]).then_inc(fb.sem, 1)
                w(dve, fb.done(ph, u))
                w(dve, ld_s.done(ph, u))
                for g in range(GP):
                    ins = dve.scalar_tensor_tensor(out=T[:, h, g, 0:D + hh], in0=carry[:, 0:D + hh], scalar=CB[:, h, g:g + 1],
                                                   in1=SIN[:, h, g, 0:D + hh], op0=ALU.mult, op1=ALU.add)
                ins.then_inc(ts.sem, 1)
                w(dve, ts.done(ph, u))
                z = [ZR[:, h, k, 0:GP * hh].rearrange("p (g k) -> p g k", k=hh) for k in range(2)]
                dve.tensor_scalar(out=z[0], in0=T[:, h, :, D:D + hh], scalar1=ZEPS if ph[1] < 2 else 0.0, scalar2=None,
                                  op0=ALU.add).then_inc(ze.sem, 1)
                w(dve, ze.done(ph, u))
                dve.reciprocal(out=z[1], in_=z[0]).then_inc(zr.sem, 1)
                w(dve, zr.done(ph, u))
                w(dve, tpa.before(ph, u))
                dve.tensor_tensor(out=ATT[:, h, :, :].rearrange("p g (k d) -> p g k d", k=hh),
                                  in0=T[:, h, :, 0:D].rearrange("p g (k d) -> p g k d", k=hh),
                                  in1=z[1].unsqueeze(3).to_broadcast([128, GP, hh, D // hh]), op=ALU.mult).then_inc(att.sem, 1)

            def update(ph):
                def body(at):
                    if ph in RAW:
                        for u in at(2):
                            squares0(ph, u)
                        for u in at(3):
                            front_a(ph, u)
                    if ph in FIX:
                        for u in at(3):
                            attention(ph, u)
                    if ph in FFN:
                        for u in at(-1):
                            squares2(ph, u)
                    if ph in RAW:
                        for u in at(2):
                            norm_x(ph, u)
                    if ph in FFN:
                        for u in at(-1):
                            norm2(ph, u)
                    else:
                        for u in at(0):
                            residual(ph, u)
                    for u in at(2):
                        h_turned(ph, u)
                    for u in at(1):
                        norm1(ph, u)
                    if ph in P1:
                        for u in at(-1):
                            residual(ph, u)
                return body

            def edges(ph):
                l = ph[1]
                hh = HEADS[l]

                def score(u):
                    w(dve, pkv.done(ph, u))
                    w(dve, qs.done(ph, u))
                    dve.tensor_tensor(out=PR[:, :, :].rearrange("p (j q) d -> p j q d", q=2), in0=psKV[:, :, :, 0:64],
                                      in1=QS[:, :, :].rearrange("p (j q) d -> p j q d", q=2), op=ALU.mult).then_inc(pr.sem, 1)
                    w(dve, pr.done(ph, u))
                    prod = PR
                    if l < 2:
                        prod = PR2
                        dve.tensor_tensor(out=PR2[:, :, :], in0=rows8(psE), in1=PR[:, :, :], op=ALU.mult).then_inc(pr2.sem, 1)
                        w(dve, pr2.done(ph, u))
                    dve.tensor_reduce(out=SC[:, 0, 0:GP * hh], in_=prod[:, :, :].rearrange("p g (k d) -> p (g k) d", k=hh),
                                      axis=AX.X, op=ALU.add).then_inc(sc.sem, 1)
                    w(dve, sc.done(ph, u))
                    scale = (D // hh) ** -0.5
                    dve.tensor_scalar(out=SC[:, 0, 0:GP * hh], in0=SC[:, 0, 0:GP * hh], scalar1=scale, scalar2=5.0,
                                      op0=ALU.mult, op1=ALU.min).then_inc(cl.sem, 1)
                    w(dve, cl.done(ph, u))
                    w(dve, ex.before(ph, u, 1))
                    dve.tensor_scalar(out=SC[:, 1, 0:GP * hh], in0=SC[:, 0, 0:GP * hh], scalar1=-5.0, scalar2=None,
                                      op0=ALU.max).then_inc(cl2.sem, 1)

                def message(u):
                    h = u.slot
                    dve.tensor_copy(CB[:, h, :], cont[:, bass.ds(u.n * GP, GP)]).then_inc(cb.sem, 1)
                    w(dve, ex.done(ph, u))
                    for q in range(2):
                        pay = PAY[:, h, :, :].rearrange("p (j q) c -> p q j c", q=2)[:, q, :, :]
                        ins = dve.tensor_tensor(out=pay[:, :, 0:D].rearrange("p j (k d) -> p j k d", k=hh),
                                                in0=psKV[:, :, q, 64:128].rearrange("p j (k d) -> p j k d", k=hh),
                                                in1=pay[:, :, D:D + hh].unsqueeze(3).to_broadcast([128, 4, hh, D // hh]),
                                                op=ALU.mult)
                    ins.then_inc(pv.sem, 1)
                    w(dve, pv.done(ph, u))
                    w(dve, cb.done(ph, u))
                    w(dve, st_s.before(ph, u))
                    for g in range(GP):
                        prev = S[:, h, g - 1, 0:D + hh] if g else S[:, 1 - h, GP - 1, 0:D + hh]
                        ins = dve.scalar_tensor_tensor(out=S[:, h, g, 0:D + hh], in0=prev, scalar=CB[:, h, g:g + 1],
                                                       in1=PAY[:, h, g, 0:D + hh], op0=ALU.mult, op1=ALU.add)
                        if g < GP - 1:
                            ins.then_inc(sweep, 1)
                            dve.wait_ge(sweep, (GP - 1) * (l * EUNITS + u.n) + g + 1)
                    ins.then_inc(sw.sem, 1)
                    w(dve, sw.done(ph, u))

                def body(at):
                    if ph in RAW:
                        for u in at(1):
                            front_a(ph, u)
                    for u in at(0):
                        score(u)
                    if ph in RAW:
                        for u in at(1):
                            squares0(ph, u)
                    for u in at(0):
                        message(u)
                    if ph in RAW:
                        for u in at(1):
                            norm_x(ph, u)
                return body

            def carry_over(l):
                hh = HEADS[l]
                dve.wait_ge(c_turn, l + 1)
                dve.tensor_tensor_scan(out=carryT[0:D + hh, 1:129], data0=throughT[0:D + hh, :],
                                       data1=banks[0:D + hh, 0, 0:128], initial=0.0, op0=ALU.mult, op1=ALU.add
                                       ).then_inc(c_scan, 1)
                dve.wait_ge(c_back, l + 1)
                dve.tensor_copy(carry[:, 0:D + hh], banks[:, 1, 0:D + hh]).then_inc(c_ready, 1)
                dve.wait_ge(c_ready, l + 1)

            for ph in PHASES:
                if ph[0] == "fix":
                    carry_over(ph[1])
                if ph[0] == "edge":
                    periods(dve, units(ph), 0, 1, edges(ph))
                else:
                    periods(dve, units(ph), -1, 3, update(ph))
                barrier(dve, ph)

        @block.tensor
        def _(pe):
            for c in owner["pe"]:
                pe.sem_inc(c.sem, 2)
            pe.wait_ge(w_loaded, 16 * N_W)
            pe.wait_ge(pool_set, 2)
            pe.wait_ge(idx_ready, 1)
            for k in range(3):
                pe.transpose(banks[:, k, 0:64], wtmp[:, k, :], ident[0:64, 0:64]).then_inc(w_turned, 1)
            pe.wait_ge(w_taken, 1)
            for l in range(2):
                ins = pe.matmul(banks[:, 4 + l, 0:1], w_1[l][0:64, :], col(f"s1{l}")[0:64, :], start=True, stop=True)
            ins.then_inc(w_turned, 1)
            for q in range(2):
                p = slice(64 * q, 64 * q + 64)
                ins = pe.matmul(banks[p, 6, 0:1], w_o[2][:, p], col("vb"), start=True, stop=True)
            ins.then_inc(w_turned, 1)
            pe.transpose(banks[0:PW, 7, 0:128], through[:, :], ident[:, :]).then_inc(w_turned, 1)
            pe.wait_ge(w_taken, 2)
            for k, name in enumerate(CENTRED):
                ins = pe.matmul(banks[:, 0, k:k + 1], center[:, :], col(name), start=True, stop=True)
            ins.then_inc(w_turned, 1)
            pe.drain().then_inc(prep, 1)
            pe.wait_ge(prep, 4)

            def turn(to, rows, h, g0=0):
                for j in range(4):
                    ins = pe.transpose(to[:, 128 * j:128 * j + 128],
                                       rows[:, h, g0 + 2 * j:g0 + 2 * j + 2, :].rearrange("p g d -> p (g d)"), ident[:, :])
                return ins

            def flat(buf, h):
                return buf[:, h, :, :].rearrange("p j n -> p (j n)")

            def tp_in(ph, u):
                w(pe, (n0 if ph in RAW else ld_n).done(ph, u))
                turn(psT[u.slot], N0, u.slot).then_inc(tp1.sem, 1)

            def tp_att(ph, u):
                w(pe, att.done(ph, u))
                turn(psC[u.slot], ATT, u.slot).then_inc(tpa.sem, 1)

            def centred(ph, u):
                w(pe, ht.done(ph, u))
                fixed = ph in FIX
                if fixed:
                    w(pe, attT.done(ph, u))
                ins = pe.matmul(psC[u.slot], (center_in if ph[1] == 1 else center)[:, :],
                                HT[:, u.slot, 0, :, :].rearrange("p j n -> p (j n)"), start=True, stop=not fixed)
                if fixed:
                    ins = pe.matmul(psC[u.slot], w_o[ph[1]][:, :], flat(ATTT, u.slot), start=False, stop=True)
                ins.then_inc(c1.sem, 1)

            def variance(ph, u):
                w(pe, sq1.done(ph, u))
                pe.matmul(psT[u.slot], mean[:, :], SQ1[:, u.slot, :], start=True, stop=True).then_inc(var1.sem, 1)

            def hidden(ph, u):
                w(pe, n1.done(ph, u))
                for q in range(2):
                    p = slice(64 * q, 64 * q + 64)
                    pe.matmul(psH[q], w_1[ph[1]][p, :], NT[p, u.slot, :], start=True, stop=True).then_inc(h1[q].sem, 1)

            def net_out(ph, u):
                pe.matmul(psZ, center_1[ph[1]][:, :], NT[:, u.slot, :], start=True, stop=True)
                w(pe, hid.done(ph, u))
                for q in range(2):
                    p = slice(64 * q, 64 * q + 64)
                    ins = pe.matmul(psZ[p, :], w_2[ph[1]][:, :], HID[:, q, :], start=False, stop=True, skip_group_check=True)
                ins.then_inc(c2.sem, 1)

            def to_rows(ph, u):
                w(pe, zt.done(ph, u))
                w(pe, (n2 if ph in FFN else res).before(ph, u, 1))
                for j in range(4):
                    ins = pe.transpose(psN[:, 128 * j:128 * j + 128], ZT[:, u.slot, j, :], ident[:, :])
                ins.then_inc(tz.sem, 1)

            def update(ph):
                def body(at):
                    for u in at(1):
                        centred(ph, u)
                    if ph in FFN:
                        for u in at(-1):
                            to_rows(ph, u)
                        for u in at(0):
                            hidden(ph, u)
                    else:
                        for u in at(0):
                            to_rows(ph, u)
                    for u in at(1):
                        variance(ph, u)
                    for u in at(2):
                        tp_in(ph, u)
                        if ph in FIX:
                            tp_att(ph, u)
                    if ph in FFN:
                        for u in at(0):
                            net_out(ph, u)
                return body

            def edges(ph):
                l = ph[1]

                def one(u):
                    h = u.slot
                    w(pe, (n0 if ph in RAW else ld_n).done(ph, u))
                    turn(psX[0], N0, h)
                    ins = turn(psX[1], N0, h, GP)
                    if l < 2:
                        w(pe, ld_ea.done(ph, u))
                        ins = turn(psX[2], EA, h)
                    ins.then_inc(tpe.sem, 1)
                    w(pe, hd.done(ph, u))
                    if l == 2:
                        pe.matmul(psQ, first_row[:, :], bias_q[:, :, :].rearrange("p g d -> p (g d)"), start=True, stop=True)
                    for j in range(4):
                        ins = pe.matmul(psQ[:, 128 * j:128 * j + 128], HT[:, 0, 1, j, :], w_q[l][:, :],
                                        start=l < 2, stop=True, skip_group_check=l == 2)
                    if l < 2:
                        w(pe, ea.done(ph, u))
                        w(pe, pr2.before(ph, u, 1))
                        for j in range(4):
                            ins = pe.matmul(psE[:, 128 * j:128 * j + 128], EAT[:, j, :], w_e[l][:, :], start=True, stop=True)
                    ins.then_inc(pq.sem, 1)
                    w(pe, pv.before(ph, u, 1))
                    if l == 2:
                        for q in range(2):
                            pe.matmul(banks[:, 3 + q, :], first_row[:, :], bias_kv[:, :, :].rearrange("p j c -> p (j c)"),
                                      start=True, stop=True)
                    for j in range(4):
                        for q in range(2):
                            p = slice(64 * q, 64 * q + 64)
                            ins = pe.matmul(banks[:, 3 + q, 128 * j:128 * j + 128], HT[p, 0, 0, j, :], w_kv[l][p, :],
                                            start=l < 2, stop=True, skip_group_check=l == 2)
                    ins.then_inc(pkv.sem, 1)

                def body(at):
                    for u in at(0):
                        one(u)
                return body

            for ph in PHASES:
                if ph[0] == "fix":
                    hh = HEADS[ph[1]]
                    pe.transpose(banks[0:D + hh, 0, 0:128], S[:, (EUNITS - 1) % 2, GP - 1, 0:D + hh], ident[:, :]).then_inc(c_turn, 1)
                    pe.wait_ge(c_scan, ph[1] + 1)
                    pe.transpose(banks[:, 1, 0:D + hh], carryT[0:D + hh, 0:128], ident[0:D + hh, 0:D + hh]).then_inc(c_back, 1)
                    pe.wait_ge(c_ready, ph[1] + 1)
                if ph[0] == "edge":
                    periods(pe, units(ph), 0, 0, edges(ph))
                else:
                    periods(pe, units(ph), -1, 2, update(ph))
                barrier(pe, ph)


_INS = ['x', 'src', 'dst', 'edge_attr_64', 'L0_gnn_WQ', 'L0_gnn_WK', 'L0_gnn_WE', 'L0_gnn_WV', 'L0_gnn_WO', 'L0_gnn_bO',
        'L0_gnn_ln1_g', 'L0_gnn_ln1_b', 'L0_gnn_W1', 'L0_gnn_b1', 'L0_gnn_W2', 'L0_gnn_b2', 'L0_gnn_ln2_g', 'L0_gnn_ln2_b',
        'L1_gnn_qk_w', 'L1_gnn_qk_b', 'L1_gnn_v_w', 'L1_gnn_v_b', 'L1_gnn_o_w', 'L1_gnn_o_b', 'L1_gnn_ln_g', 'L1_gnn_ln_b']


def kernel(**inputs):
    import numpy as _np
    import concourse.bacc as _bacc
    from concourse import mybir as _mybir
    from concourse.bass_utils import run_bass_kernel_spmd as _run

    nc = _bacc.Bacc("TRN2", target_bir_lowering=False, num_devices=1)
    arrays, args = {}, []
    for name in _INS:
        a = _np.ascontiguousarray(inputs[name])
        arrays[f"in_{name}_dram"] = a
        args.append(nc.dram_tensor(f"in_{name}_dram", a.shape, _mybir.dt.from_np(a.dtype), kind="ExternalInput").ap())
    args.append(nc.dram_tensor("out_0_dram", (N, D), _mybir.dt.float32, kind="ExternalOutput").ap())
    build(nc, *args)
    r = _run(nc, [arrays], core_ids=[0])
    return r.results[0]["out_0_dram"]
```

```python
import concourse.bass as bass
from concourse import mybir
from contextlib import ExitStack

N, D, E = 100000, 64, 25000
HEADS = (4, 4, 1)
GP = 8
ROWS = 128 * GP
UNITS = -(-N // ROWS)
TAIL = (N - (UNITS - 1) * ROWS) // GP
EP, ET = 125, 200
EUNITS = ET // GP
PW = D + 4
EPS, ZEPS = 1e-5, 1e-6
LN_EXP_SET = 6
FAR = 1 << 20

PHASES = [(kind, layer) for layer in range(3) for kind in ("dense", "edge", "fix")]
RAW = [(k, l) for k, l in PHASES if l != 1 and k != "fix"]


def units(phase):
    return UNITS if phase[0] == "dense" else EUNITS


class Count:

    def __init__(self, sem, phases):
        self.sem, self.base, at = sem, {}, 2
        for ph in PHASES:
            self.base[ph] = at
            at += units(ph) if ph in phases else 0

    def done(self, ph, u):
        return self.sem, self.base[ph] + u.n + 1

    def before(self, ph, u, back=2):
        return self.sem, self.base[ph] + u.n + 1 - back


class Slots:

    def __init__(self, sems, phases):
        self.sems, self.base, at = sems, {}, [0, 0]
        for ph in PHASES:
            self.base[ph] = tuple(at)
            if ph in phases:
                at = [at[h] + 16 * ((units(ph) + 1 - h) // 2) for h in range(2)]

    def done(self, ph, u):
        return self.sems[u.slot], self.base[ph][u.slot] + 16 * (u.turn + 1)

    def before(self, ph, u):
        return self.sems[u.slot], self.base[ph][u.slot] + 16 * u.turn


class Unit:

    def __init__(self, pair, off):
        self.n, self.slot, self.turn = 2 * pair + off, off % 2, pair + off // 2


def periods(eng, count, lo, hi, body):
    def written(u):
        body(lambda k: [Unit(0, u + k)] if 0 <= u + k < count else [])

    first = -(lo // 2) if lo < 0 else 0
    end = max(first, (count - hi) // 2)
    for u in range(-hi, 2 * first):
        written(u)
    if end - first > 1:
        with eng.Fori(first, end) as i:
            for s in range(2):
                body(lambda k, s=s: [Unit(i, s + k)])
    else:
        end = first
    for u in range(2 * end, count - lo):
        written(u)


def build(nc, x, src, dst, edge_attr, WQ, WK, WE, WV, WO, bO, ln1_g, ln1_b, W1, b1, W2, b2, ln2_g, ln2_b,
          qk_w, qk_b, v_w, v_b, o_w, o_b, ln_g, ln_b, out):
    f32, i32 = mybir.dt.float32, mybir.dt.int32
    ALU, ACT, AX = mybir.AluOpType, mybir.ActivationFunctionType, mybir.AxisListType
    ctx = ExitStack()
    with ctx:
        ctx.enter_context(nc.allow_non_contiguous_dma(reason="columns of biases, and single edges"))

        def sb(name, shape, dt=f32):
            return ctx.enter_context(nc.sbuf_tensor(name, shape, dt))

        def pb(name, shape):
            return ctx.enter_context(nc.psum_tensor(name, shape, f32))

        def sem(name):
            return ctx.enter_context(nc.semaphore(name))

        def dram(name, shape):
            return nc.dram_tensor(name, shape, f32)

        normed1 = dram("normed1", [N, D])
        x1 = dram("x1", [N, D])
        ends = [dram(f"ends{l}", [EUNITS, 128, 2 * GP, D]) for l in range(3)]
        targets = [dram(f"targets{l}", [EUNITS, 128, GP, D]) for l in range(3)]
        sums = [dram(f"sums{l}", [EUNITS, 128, PW, GP]) for l in range(3)]
        table = [x, normed1, x1]
        result = [normed1, x1, out]

        ident = sb("ident", [128, 128])
        center = sb("center", [128, 128])
        mean = sb("mean", [128, 128])
        center_in = sb("center_in", [128, 128])
        center_1 = [sb(f"center_1{l}", [128, 128]) for l in range(2)]
        heads = [sb(f"heads{k}", [128, 2 * n]) for k, n in enumerate((4, 1))]
        WKS, WVS, WQS, WES, WOS = (sb(name, [128, n, 128]) for name, n in
                                   (("w_k", 2), ("w_v", 3), ("w_q", 3), ("w_e", 2), ("w_o", 3)))
        W1S, W2S = sb("w_1", [128, 2, 128]), sb("w_2", [128, 2, 64])
        w_k, w_v, w_q, w_e, w_o, w_1, w_2 = ([b[:, l, :] for l in range(b.shape[1])]
                                             for b in (WKS, WVS, WQS, WES, WOS, W1S, W2S))
        wtmp = sb("wtmp", [64, 3, 128])
        wsum = sb("wsum", [128, 8])
        vec = sb("vec", [128, 32])
        names = {}

        CENTRED = {"bO0": "cb0", "in1": "cb1", "ob": "cb2", "obf": "cbf", "y0": "zb0", "y1": "zb1"}

        def col(name):
            k = names.setdefault(name, len(names))
            return vec[:, k:k + 1]

        eps_col = col("eps")

        src_i = sb("src_i", [128, ET], i32)
        dst_i = sb("dst_i", [128, ET], i32)
        prev_i = sb("prev_i", [128, 1], i32)
        next_i = sb("next_i", [128, 1], i32)
        dst_f = sb("dst_f", [128, ET])
        shift_f = sb("shift_f", [128, ET])
        far_f = sb("far_f", [128, ET])
        zero_f = sb("zero_f", [128, ET])
        cont = sb("cont", [128, ET])
        inner = sb("inner", [128, ET])
        head = sb("head", [128, ET])
        gidx = sb("gidx", [128, EUNITS, 2 * GP], i32)
        sidx = sb("sidx", [128, ET], i32)
        through = sb("through", [128, PW])
        throughT = sb("throughT", [PW, 128])
        carryT = sb("carryT", [PW, 136])
        carry = sb("carry", [128, PW])

        X = sb("X", [128, 2, 2 * GP, D])
        XM = sb("XM", [128, 2, 2 * GP, D])
        SQ0 = sb("SQ0", [128, 2, 2 * GP, D])
        N0 = sb("N0", [128, 2, 2 * GP, D])
        HT = sb("HT", [128, 2, 2, 4, 128])
        SQ1 = sb("SQ1", [128, 2, 512])
        LG1 = sb("LG1", [128, 512])
        R1 = sb("R1", [128, 2, 512])
        NT = sb("NT", [128, 2, 512])
        HID = sb("HID", [128, 2, 512])
        ZT = sb("ZT", [128, 2, 4, 128])
        SQ2 = sb("SQ2", [128, 2, GP, D])
        N2 = sb("N2", [128, 2, GP, D])
        NG = sb("NG", [128, GP, D])
        XS = sb("XS", [128, GP, D])
        gain_row = sb("gain_row", [128, D])
        shift_row = sb("shift_row", [128, D])
        OUT = sb("OUT", [128, 2, GP, D])
        X2 = sb("X2", [128, 2, GP, D])
        EA = sb("EA", [128, 2, GP, D])
        EAT = sb("EAT", [128, 2, 4, 128])
        QS = sb("QS", [128, 512])
        PR = sb("PR", [128, 512])
        PR2 = sb("PR2", [128, 512])
        SC = sb("SC", [128, GP * 4])
        PAY = sb("PAY", [128, 2, PW, GP])
        FL = sb("FL", [128, 2, PW, GP])
        S = sb("S", [128, 2, PW, GP])
        SIN = sb("SIN", [128, 2, PW, GP])
        T = sb("T", [128, 2, PW, GP])
        ZR = sb("ZR", [128, 2, 2, 4, GP])
        ATT = sb("ATT", [128, 2, GP, D])
        ATTT = sb("ATTT", [128, 2, 4, 128])
        CB = sb("CB", [128, 2, GP])
        IN = sb("IN", [128, 2, GP])
        st0 = sb("st0", [128, 2, 5, 2 * GP])
        st2 = sb("st2", [128, 2, 4, GP])
        GB = sb("GB", [128, 2, 2 * GP, D])
        IB = sb("IB", [128, 2, 2 * GP], i32)

        banks = pb("banks", [128, 8, 512])
        psT = [banks[:, h, :] for h in range(2)]
        psC = [banks[:, 2 + h, :] for h in range(2)]
        psH = [banks[:, 4 + q, :] for q in range(2)]
        psZ, psN = banks[:, 6, :], banks[:, 7, :]
        psX = [banks[:, k, :] for k in range(3)]
        psQ, psK, psE, psV = (banks[:, k, :] for k in range(3, 7))
        psS = banks[:, 7, 0:GP * 4]

        def rows8(ap):
            return ap.rearrange("p (g d) -> p g d", d=D)

        DENSE = [("dense", l) for l in range(3)]
        EDGE = [("edge", l) for l in range(3)]
        FIX = [("fix", l) for l in range(3)]
        UPD = DENSE + FIX
        FFN = [p for p in UPD if p[1] < 2]
        BACK = [p for p in UPD if p[1] > 0]
        P1 = [p for p in UPD if p[1] == 1]
        owner = {"dve": [], "act": [], "pe": [], "pool": []}

        def count(eng, name, phases):
            c = Count(sem(name), phases)
            owner[eng].append(c)
            return c

        x_summed = count("dve", "x_summed", RAW)
        x_centred = count("dve", "x_centred", RAW)
        x_squared = count("act", "x_squared", RAW)
        x_squares_summed = count("dve", "x_squares_summed", RAW)
        x_variance_logged = count("act", "x_variance_logged", RAW)
        x_rstd_ready = count("act", "x_rstd_ready", RAW)
        x_normed = count("dve", "x_normed", RAW)
        rows_turned = count("pe", "rows_turned", UPD)
        turned_rows_kept = count("dve", "turned_rows_kept", UPD)
        centred_ready = count("pe", "centred_ready", UPD)
        centred_squared = count("act", "centred_squared", UPD)
        variance_ready = count("pe", "variance_ready", UPD)
        variance_logged = count("act", "variance_logged", UPD)
        rstd_ready = count("act", "rstd_ready", UPD)
        normed_before_net = count("dve", "normed_before_net", UPD)
        hidden_in_psum = [count("pe", f"hidden_in_psum{q}", FFN) for q in range(2)]
        hidden_ready = count("act", "hidden_ready", FFN)
        net_ready = count("pe", "net_ready", FFN)
        out_kept = count("act", "out_kept", UPD)
        out_turned = count("pe", "out_turned", UPD)
        out_squared = count("act", "out_squared", FFN)
        out_squares_summed = count("dve", "out_squares_summed", FFN)
        out_variance_logged = count("act", "out_variance_logged", FFN)
        out_rstd_ready = count("act", "out_rstd_ready", FFN)
        out_normed = count("dve", "out_normed", FFN)
        gain_applied = count("dve", "gain_applied", P1)
        residual_shifted = count("dve", "residual_shifted", P1)
        residual_added = count("dve", "residual_added", BACK)
        heads_copied = count("dve", "heads_copied", FIX)
        scatter_idx_ready = count("dve", "scatter_idx_ready", FIX)
        whole_sums_ready = count("dve", "whole_sums_ready", FIX)
        weight_sums_ready = count("dve", "weight_sums_ready", FIX)
        weight_sums_inverted = count("dve", "weight_sums_inverted", FIX)
        attention_ready = count("dve", "attention_ready", FIX)
        attention_in_psum = count("pe", "attention_in_psum", FIX)
        attention_kept = count("act", "attention_kept", FIX)
        ends_in_psum = count("pe", "ends_in_psum", EDGE)
        sources_kept = count("act", "sources_kept", EDGE)
        targets_kept = count("act", "targets_kept", EDGE)
        edge_rows_kept = count("act", "edge_rows_kept", EDGE[:2])
        queries_ready = count("pe", "queries_ready", EDGE)
        keys_ready = count("pe", "keys_ready", EDGE)
        edge_factors_ready = count("pe", "edge_factors_ready", EDGE[:2])
        values_ready = count("pe", "values_ready", EDGE)
        queries_kept = count("act", "queries_kept", EDGE)
        key_query_ready = count("dve", "key_query_ready", EDGE)
        factors_ready = count("dve", "factors_ready", EDGE[:2])
        scores_ready = count("pe", "scores_ready", EDGE)
        scores_clipped = count("dve", "scores_clipped", EDGE)
        weights_ready = count("act", "weights_ready", EDGE)
        mean_ready = count("act", "mean_ready", [EDGE[0], EDGE[2]])
        flags_copied = count("pool", "flags_copied", EDGE)
        flags_spread = count("act", "flags_spread", EDGE)
        messages_ready = count("dve", "messages_ready", EDGE)
        carried_on = count("dve", "carried_on", EDGE)
        sums_ready = count("dve", "sums_ready", EDGE)

        def slots(name, phases):
            return Slots([sem(f"{name}{h}") for h in range(2)], phases)

        x_loaded = slots("x_loaded", RAW)
        rows_loaded = slots("rows_loaded", [p for p in PHASES if p not in RAW])
        residual_loaded = slots("residual_loaded", BACK)
        edge_rows_loaded = slots("edge_rows_loaded", EDGE[:2])
        sums_loaded = slots("sums_loaded", FIX)
        rows_stored = slots("rows_stored", DENSE)
        targets_stored_in = [EDGE[0], EDGE[2]]
        targets_stored = slots("targets_stored", targets_stored_in)
        sums_stored = slots("sums_stored", EDGE)
        scattered = slots("scattered", FIX)
        gathered = [sem(f"gathered{h}") for h in range(2)]
        ends_out = [sem(f"ends_out{h}") for h in range(2)]
        idx_copied = sem("idx_copied")
        phase_end = sem("phase_end")
        w_loaded, m_loaded, ones_set, prep = sem("w_loaded"), sem("m_loaded"), sem("ones_set"), sem("prep")
        pool_set, passed = sem("pool_set"), sem("passed")
        w_turned, w_taken = sem("w_turned"), sem("w_taken")
        e_loaded, idx_ready = sem("e_loaded"), sem("idx_ready")
        last_sums_turned, carry_scanned = sem("last_sums_turned"), sem("carry_scanned")
        carry_turned, carry_ready = sem("carry_turned"), sem("carry_ready")

        def shift1(ph):
            return col("cbf") if ph == ("fix", 2) else col(f"cb{ph[1]}")

        def last(ph):
            return residual_added if ph in BACK else out_normed

        def leaving(ph):
            return OUT if ph in BACK else N2

        def barrier(eng, ph):
            eng.drain().then_inc(phase_end, 1)
            eng.wait_ge(phase_end, 5 * (PHASES.index(ph) + 1))

        wide = {ph: (2 if ph[0] == "edge" else 1) * GP for ph in PHASES}

        def w(eng, what):
            eng.wait_ge(*what)

        pairs = [("bO", bO), ("g1", ln1_g), ("s1", ln1_b), ("b2", b2), ("g2", ln2_g), ("s2", ln2_b)]
        vectors = [("qkb", qk_b), ("ob", o_b), ("vb", v_b), ("lg", ln_g), ("ls", ln_b)]
        for name in [f"{name}{l}" for name, _ in pairs for l in range(2)] + [name for name, _ in vectors]:
            col(name)
        for l in range(2):
            col(f"fb{l}")
        for l in range(2):
            col(f"y{l}")
            col(f"zb{l}")
        for name in ("in1", "obf", "cb0", "cb1", "cb2", "cbf"):
            col(name)
        N_W = 2 * (len(pairs) + len(vectors)) + 1 + 2 * 3 + 2
        N_M = 2 * 6 + 1
        assert names["fb1"] == names["fb0"] + 1

        block = ctx.enter_context(nc.Block())

        @block.sync
        def _(sp):
            sp.wait_ge(ones_set, 1)
            sp.dma_start(src_i[0:EP, :], src.rearrange("(p t) -> p t", t=ET)).then_inc(e_loaded, 16)
            sp.dma_start(dst_i[0:EP, :], dst.rearrange("(p t) -> p t", t=ET)).then_inc(e_loaded, 16)
            grid = dst.rearrange("(p t) -> p t", t=ET)
            sp.dma_start(prev_i[1:EP, :], grid[0:EP - 1, ET - 1:ET]).then_inc(e_loaded, 16)
            sp.dma_start(next_i[0:EP - 1, :], grid[1:EP, 0:1]).then_inc(e_loaded, 16)
            def load(to, what):
                sp.dma_start(to, what).then_inc(w_loaded, 16)

            sp.wait_ge(ones_set, 2)
            for q in range(2):
                p = slice(64 * q, 64 * q + 64)
                for name, v in pairs:
                    k = names[f"{name}0"]
                    load(vec[p, k:k + 2], v.rearrange("l p -> p l"))
                for name, v in vectors:
                    load(col(name)[p, :], v.rearrange("(p a) -> p a", a=1))
            load(vec[:, names["fb0"]:names["fb0"] + 2], b1.rearrange("l p -> p l"))
            for k, m in enumerate((qk_w, v_w, o_w)):
                for q in range(2):
                    load(wtmp[:, k, 64 * q:64 * q + 64], m)
            load(gain_row[:, :], ln2_g[1:2, :].to_broadcast([128, D]))
            load(shift_row[:, :], ln2_b[1:2, :].to_broadcast([128, D]))

            def node_rows(t, n, parts=slice(0, 128)):
                m = parts.stop - parts.start
                return t[bass.ds(n * ROWS + parts.start * GP, m * GP), :].rearrange("(p g) d -> p g d", g=GP)

            def part(ph, u):
                return slice(0, TAIL if ph[0] == "dense" and isinstance(u.n, int) and u.n == UNITS - 1 else 128)

            early = []

            def started(load_, u):
                return isinstance(u.n, int) and (load_, u.n) in early

            def load_x(ph, u):
                if started(load_x, u):
                    return
                p, h = part(ph, u), u.slot
                w(sp, x_centred.before(ph, u))
                if ph[0] == "dense":
                    sp.dma_start(X[p, h, 0:GP, :], node_rows(table[ph[1]], u.n, p)).then_inc(x_loaded.sems[h], 16)
                else:
                    sp.dma_start(X[:, h, :, :], ends[ph[1]][u.n, :, :, :]).then_inc(x_loaded.sems[h], 16)

            def load_n(ph, u):
                if started(load_n, u):
                    return
                p, h = part(ph, u), u.slot
                w(sp, (ends_in_psum if ph[0] == "edge" else rows_turned).before(ph, u))
                if ph[0] == "dense":
                    sp.dma_start(N0[p, h, 0:GP, :], node_rows(normed1, u.n, p)).then_inc(rows_loaded.sems[h], 16)
                elif ph[0] == "edge":
                    sp.dma_start(N0[:, h, :, :], ends[1][u.n, :, :, :]).then_inc(rows_loaded.sems[h], 16)
                elif ph[1] == 1:
                    sp.dma_start(N0[:, h, 0:GP, :], ends[1][u.n, :, GP:2 * GP, :]).then_inc(rows_loaded.sems[h], 16)
                else:
                    sp.dma_start(N0[:, h, 0:GP, :], targets[ph[1]][u.n, :, :, :]).then_inc(rows_loaded.sems[h], 16)

            def load_r(ph, u):
                p, h = part(ph, u), u.slot
                w(sp, residual_added.before(ph, u))
                if ph[0] == "dense":
                    sp.dma_start(X2[p, h, :, :], node_rows(x if ph[1] == 1 else x1, u.n, p)
                        ).then_inc(residual_loaded.sems[h], 16)
                else:
                    sp.dma_start(X2[:, h, :, :], ends[0 if ph[1] == 1 else 2][u.n, :, GP:2 * GP, :]
                        ).then_inc(residual_loaded.sems[h], 16)

            def load_ea(ph, u):
                if started(load_ea, u):
                    return
                w(sp, ends_in_psum.before(ph, u))
                e3 = edge_attr.rearrange("(p t) d -> p t d", t=ET)
                sp.dma_start(EA[0:EP, u.slot, :, :], e3[:, bass.ds(u.n * GP, GP), :]
                    ).then_inc(edge_rows_loaded.sems[u.slot], 16)

            def load_s(ph, u):
                if started(load_s, u):
                    return
                w(sp, whole_sums_ready.before(ph, u))
                sp.dma_start(SIN[:, u.slot, :, :], sums[ph[1]][u.n, :, :, :]).then_inc(sums_loaded.sems[u.slot], 16)

            def store_rows(ph, u):
                p, h = part(ph, u), u.slot
                w(sp, last(ph).done(ph, u))
                sp.dma_start(node_rows(result[ph[1]], u.n, p), leaving(ph)[p, h, :, :]).then_inc(rows_stored.sems[h], 16)

            def store_sums(ph, u):
                w(sp, sums_ready.done(ph, u))
                sp.dma_start(sums[ph[1]][u.n, :, :, :], S[:, u.slot, :, :]).then_inc(sums_stored.sems[u.slot], 16)

            def store_targets(ph, u):
                w(sp, x_normed.done(ph, u))
                sp.dma_start(targets[ph[1]][u.n, :, :, :], N0[:, u.slot, GP:2 * GP, :]
                    ).then_inc(targets_stored.sems[u.slot], 16)

            def update(ph):
                end = -1 if ph in FFN else 0

                def body(at):
                    if ph in RAW:
                        for u in at(6 if ph[1] == 2 else 5):
                            load_x(ph, u)
                    else:
                        for u in at(4):
                            load_n(ph, u)
                    if ph in FIX:
                        for u in at(5):
                            load_s(ph, u)
                    if ph in DENSE:
                        for u in at(end):
                            store_rows(ph, u)
                    if ph in BACK:
                        for u in at(end + 2):
                            load_r(ph, u)
                return body

            def edges(ph):
                def body(at):
                    if ph in RAW:
                        for u in at(5):
                            load_x(ph, u)
                        for u in at(1):
                            store_targets(ph, u)
                    for u in at(3):
                        if ph not in RAW:
                            load_n(ph, u)
                        if ph[1] < 2:
                            load_ea(ph, u)
                    for u in at(-1):
                        store_sums(ph, u)
                return body

            def stored(slot, ph):
                for h in range(2):
                    w(sp, slot.done(ph, Unit((units(ph) + 1 - h) // 2 - 1, h)))

            def start_early(ph, *loads):
                for load_ in loads:
                    for k in range(2):
                        load_(ph, Unit(0, k))
                        early.append((load_, k))

            def ahead(ph):
                early.clear()
                l = ph[1]
                if ph[0] == "edge":
                    for h in range(2):
                        sp.wait_ge(ends_out[h], 16 * (l + 1) * ((EUNITS + 1 - h) // 2))
                    read = x_centred if ph in RAW else rows_turned
                    sp.wait_ge(read.sem, read.base[ph])
                    start_early(ph, load_x if ph in RAW else load_n)
                    if l < 2:
                        start_early(ph, load_ea)
                if ph[0] == "fix":
                    if ("edge", l) in targets_stored_in:
                        stored(targets_stored, ("edge", l))
                    for k in (EUNITS - 1, EUNITS):
                        w(sp, sums_stored.before(("edge", l), Unit(0, k)))
                    start_early(ph, load_s)
                    sp.wait_ge(ends_in_psum.sem, ends_in_psum.base[ph])
                    start_early(ph, load_n)

            def run(ph):
                k = PHASES.index(ph)
                if ph[0] == "fix":
                    stored(sums_stored, ("edge", ph[1]))
                if ph[0] == "edge":
                    periods(sp, units(ph), -1, 5, edges(ph))
                    stored(rows_stored, ("dense", ph[1]))
                else:
                    periods(sp, units(ph), -1, 7, update(ph))
                if k + 1 < len(PHASES):
                    ahead(PHASES[k + 1])
                barrier(sp, ph)

            sp.wait_ge(ones_set, 3)
            start_early(PHASES[0], load_x)
            sp.wait_ge(prep, 4)
            for ph in PHASES:
                run(ph)

        @block.gpsimd
        def _(pool):
            for c in owner["pool"]:
                pool.sem_inc(c.sem, 2)
            pool.memset(ident[:, :], 0.0).then_inc(pool_set, 1)
            pool.wait_ge(pool_set, 1)
            pool.affine_select(out=ident[:, :], in_=ident[:, :], compare_op=ALU.not_equal, fill=1.0,
                               base=0, pattern=[[-1, 128]], channel_multiplier=1).then_inc(pool_set, 1)
            pool.wait_ge(ones_set, 2)
            for q in range(2):
                p = slice(64 * q, 64 * q + 64)
                for to, m in ((WKS, WK), (WVS, WV), (WQS, WQ), (WES, WE), (WOS, WO)):
                    pool.dma_start(to[p, 0:2, p], m.rearrange("l a b -> a l b")).then_inc(m_loaded, 16)
                pool.dma_start(W1S[p, :, :], W1.rearrange("l a b -> a l b")).then_inc(m_loaded, 16)
            pool.dma_start(W2S[:, :, :], W2.rearrange("l a b -> a l b")).then_inc(m_loaded, 16)
            pool.wait_ge(idx_ready, 1)
            pool.drain().then_inc(prep, 1)

            def hold(sem_, value):
                pool.wait_ge(sem_, value)
                pool.sem_inc(passed, 1)

            def gather(l):
                before = l * EUNITS

                def fetch(u, h, k, *unit_before):
                    if l or not (isinstance(k, int) and k == 0):
                        hold(ends_out[h], 16 * (k + l * ((EUNITS + 1 - h) // 2)))
                    pool.tensor_copy(IB[:, h, :], gidx[:, bass.ds(u, 1), :].rearrange("p a k -> p (a k)")
                        ).then_inc(idx_copied, 1)
                    hold(idx_copied, before + u + 1)
                    for g in range(2 * GP):
                        if g == GP // 2 and unit_before:
                            put(*unit_before)
                        pool.indirect_dma_start(out=GB[:, h, g, :], out_offset=None, in_=table[l][:, :],
                                                in_offset=bass.IndirectOffsetOnAxis(ap=IB[:, h, g:g + 1], axis=0)
                                                ).then_inc(gathered[h], 16)

                def put(u, h, k):
                    hold(gathered[h], 16 * 2 * GP * (k + 1 + l * ((EUNITS + 1 - h) // 2)))
                    pool.dma_start(ends[l][u, :, :, :], GB[:, h, :, :]).then_inc(ends_out[h], 16)

                fetch(0, 0, 0)
                with pool.Fori(0, EUNITS // 2) as i:
                    fetch(2 * i + 1, 1, i, 2 * i, 0, i)
                    fetch(2 * i + 2, 0, i + 1, 2 * i + 1, 1, i)
                put(EUNITS - 1, 0, EUNITS // 2)
                for h in range(2):
                    pool.wait_ge(ends_out[h], 16 * (l + 1) * ((EUNITS + 1 - h) // 2))

            def scatter(ph):
                def scatter_unit(i, h):
                    u = Unit(i, h)
                    hold(*scatter_idx_ready.done(ph, u))
                    hold(*last(ph).done(ph, u))
                    for g in range(GP):
                        pool.indirect_dma_start(out=result[ph[1]][:, :],
                                                out_offset=bass.IndirectOffsetOnAxis(ap=IB[:, h, g:g + 1], axis=0),
                                                in_=leaving(ph)[:, h, g, :], in_offset=None,
                                                bounds_check=N - 1, oob_is_err=False).then_inc(scattered.sems[h], 16)

                with pool.Fori(0, EUNITS // 2) as i:
                    scatter_unit(i, 0)
                    scatter_unit(i, 1)
                scatter_unit(EUNITS // 2, 0)
                for h in range(2):
                    pool.wait_ge(scattered.sems[h], GP * (scattered.base[ph][h] + 16 * ((EUNITS + 1 - h) // 2)))

            def flags(ph, u):
                hold(*sums_ready.before(ph, u))
                pool.tensor_copy(CB[:, u.slot, :], cont[:, bass.ds(u.n * GP, GP)])
                pool.tensor_copy(IN[:, u.slot, :], inner[:, bass.ds(u.n * GP, GP)]).then_inc(flags_copied.sem, 1)

            def norm_x(ph, u):
                g, h = 2 * GP, u.slot
                hold(*x_rstd_ready.done(ph, u))
                hold(*ends_in_psum.before(ph, u))
                hold(*targets_stored.before(ph, u))
                pool.tensor_tensor(out=N0[:, h, :, :], in0=XM[:, h, :, :],
                                   in1=st0[:, h, 3, :].unsqueeze(2).to_broadcast([128, g, D]), op=ALU.mult
                                   ).then_inc(x_normed.sem, 1)

            def centre_x(ph, u):
                h = u.slot
                hold(*x_loaded.done(ph, u))
                hold(*mean_ready.done(ph, u))
                hold(*x_normed.before(ph, u))
                pool.tensor_tensor(out=XM[:, h, :, :], in0=X[:, h, :, :],
                                   in1=st0[:, h, 4, :].unsqueeze(2).to_broadcast([128, 2 * GP, D]), op=ALU.add
                                   ).then_inc(x_centred.sem, 1)

            def edges(ph):
                def body(at):
                    for u in at(0):
                        flags(ph, u)
                    if ph in RAW:
                        for u in at(3):
                            centre_x(ph, u)
                        for u in at(2):
                            norm_x(ph, u)
                return body

            for ph in PHASES:
                if ph[0] == "dense":
                    gather(ph[1])
                if ph[0] == "edge":
                    periods(pool, EUNITS, 0, 3, edges(ph))
                if ph[0] == "fix":
                    scatter(ph)
                barrier(pool, ph)

        @block.scalar
        def _(act):
            act.add_instruction(mybir.InstLoadActFuncSet(name=nc.get_next_instruction_name(), act_func_set_id=LN_EXP_SET,
                                                         engine=mybir.EngineType.Activation))
            for c in owner["act"]:
                act.sem_inc(c.sem, 2)
            act.drain().then_inc(prep, 1)
            act.wait_ge(prep, 4)

            def square0(ph, u):
                g = wide[ph]
                w(act, x_centred.done(ph, u))
                act.activation(SQ0[:, u.slot, 0:g, :], XM[:, u.slot, 0:g, :], ACT.Square).then_inc(x_squared.sem, 1)

            def rstd(ph, u, st, g, ss, lg, r):
                h = u.slot
                w(act, ss.done(ph, u))
                act.activation(st[:, h, 2, 0:g], st[:, h, 1, 0:g], ACT.Ln, bias=eps_col, scale=1.0 / D).then_inc(lg.sem, 1)
                w(act, lg.done(ph, u))
                act.activation(st[:, h, 3, 0:g], st[:, h, 2, 0:g], ACT.Exp, scale=-0.5).then_inc(r.sem, 1)

            def square1(ph, u):
                w(act, centred_ready.done(ph, u))
                act.activation(SQ1[:, u.slot, :], psC[u.slot], ACT.Square, bias=shift1(ph)).then_inc(centred_squared.sem, 1)

            def rstd1(ph, u):
                w(act, variance_ready.done(ph, u))
                act.activation(LG1[:, :], psT[u.slot], ACT.Ln, bias=eps_col).then_inc(variance_logged.sem, 1)
                w(act, variance_logged.done(ph, u))
                act.activation(R1[:, u.slot, :], LG1[:, :], ACT.Exp, scale=-0.5).then_inc(rstd_ready.sem, 1)

            def hidden(ph, u):
                for q in range(2):
                    w(act, hidden_in_psum[q].done(ph, u))
                    ins = act.activation(HID[:, q, :], psH[q], ACT.Relu, bias=col(f"fb{ph[1]}"), scale=1.0)
                ins.then_inc(hidden_ready.sem, 1)

            def turned_out(ph, u):
                h = u.slot
                to = ZT[:, h, :, :].rearrange("p j n -> p (j n)")
                if ph in FFN:
                    w(act, net_ready.done(ph, u))
                    ins = act.activation(to, psZ, ACT.Identity, bias=col(f"zb{ph[1]}"), scale=1.0)
                else:
                    w(act, normed_before_net.done(ph, u))
                    w(act, out_turned.before(ph, u))
                    ins = act.activation(to, NT[:, h, :], ACT.Identity, bias=col("ls"), scale=col("lg"))
                ins.then_inc(out_kept.sem, 1)

            def square2(ph, u):
                w(act, out_turned.done(ph, u))
                act.activation(SQ2[:, u.slot, :, :], rows8(psN), ACT.Square).then_inc(out_squared.sem, 1)

            def att_turned(ph, u):
                w(act, attention_in_psum.done(ph, u))
                act.activation(ATTT[:, u.slot, :, :].rearrange("p j n -> p (j n)"), psC[u.slot], ACT.Copy
                    ).then_inc(attention_kept.sem, 1)

            def update(ph):
                end = -1 if ph in FFN else 0

                def last_layer(at):
                    for u in at(1):
                        square1(ph, u)
                    for u in at(0):
                        turned_out(ph, u)
                    for u in at(3):
                        rstd(ph, u, st0, GP, x_squares_summed, x_variance_logged, x_rstd_ready)
                    for u in at(1):
                        rstd1(ph, u)
                    for u in at(4):
                        square0(ph, u)

                def body(at):
                    for u in at(end):
                        turned_out(ph, u)
                    for u in at(1):
                        square1(ph, u)
                    if ph in FFN:
                        for u in at(-1):
                            square2(ph, u)
                    if ph in RAW:
                        for u in at(2):
                            rstd(ph, u, st0, GP, x_squares_summed, x_variance_logged, x_rstd_ready)
                    if ph in FFN:
                        for u in at(0):
                            hidden(ph, u)
                        for u in at(-1):
                            rstd(ph, u, st2, GP, out_squares_summed, out_variance_logged, out_rstd_ready)
                    for u in at(1):
                        rstd1(ph, u)
                    if ph in FIX:
                        for u in at(2):
                            att_turned(ph, u)
                    if ph in RAW:
                        for u in at(3):
                            square0(ph, u)
                return last_layer if ph == ("dense", 2) else body

            def edges(ph):
                l = ph[1]
                hh = HEADS[l]

                def mean_x(u):
                    w(act, x_summed.done(ph, u))
                    act.activation(st0[:, u.slot, 4, :], st0[:, u.slot, 0, :], ACT.Copy, scale=-1.0 / D
                        ).then_inc(mean_ready.sem, 1)

                def flags(u):
                    w(act, flags_copied.done(ph, u))
                    w(act, sums_ready.before(ph, u))
                    act.activation(FL[:, u.slot, :, :], IN[:, u.slot, :].unsqueeze(1).to_broadcast([128, PW, GP]),
                                   ACT.Copy).then_inc(flags_spread.sem, 1)

                def queries(u):
                    w(act, queries_ready.done(ph, u))
                    if l < 2:
                        act.activation(QS[:, :], psQ, ACT.Copy).then_inc(queries_kept.sem, 1)
                    else:
                        act.activation(QS[:, :], psQ, ACT.Identity, bias=col("qkb"), scale=1.0
                            ).then_inc(queries_kept.sem, 1)

                def weights(u):
                    w(act, scores_clipped.done(ph, u))
                    act.activation(PAY[:, u.slot, D:D + hh, :].rearrange("p k g -> p g k"),
                                   SC[:, 0:GP * hh].rearrange("p (g k) -> p g k", k=hh), ACT.Exp
                                       ).then_inc(weights_ready.sem, 1)

                def ends_turned(u):
                    w(act, ends_in_psum.done(ph, u))
                    for k, s_ in ((1, targets_kept), (0, sources_kept)):
                        to = HT[:, u.slot, k, :, :].rearrange("p j n -> p (j n)")
                        if l == 1:
                            act.activation(to, psX[k], ACT.Identity, bias=col("s20"), scale=col("g20")).then_inc(s_.sem, 1)
                        else:
                            act.activation(to, psX[k], ACT.Relu).then_inc(s_.sem, 1)
                    if l < 2:
                        act.activation(EAT[:, u.slot, :, :].rearrange("p j n -> p (j n)"), psX[2], ACT.Copy
                            ).then_inc(edge_rows_kept.sem, 1)

                def body(at):
                    for u in at(-1):
                        weights(u)
                    for u in at(0):
                        queries(u)
                    if ph in RAW:
                        for u in at(3):
                            mean_x(u)
                    for u in at(0):
                        flags(u)
                    if ph in RAW:
                        for u in at(2):
                            rstd(ph, u, st0, 2 * GP, x_squares_summed, x_variance_logged, x_rstd_ready)
                    for u in at(1):
                        ends_turned(u)
                    if ph in RAW:
                        for u in at(3):
                            square0(ph, u)
                return body

            for ph in PHASES:
                if ph[0] == "edge":
                    periods(act, units(ph), -1, 3, edges(ph))
                else:
                    periods(act, units(ph), -1, 4, update(ph))
                barrier(act, ph)

        @block.vector
        def _(dve):
            for c in owner["dve"]:
                dve.sem_inc(c.sem, 2)
            done = [0]

            def step(ins):
                done[0] += 1
                ins.then_inc(ones_set, 1)
                return done[0]

            def chain(ins):
                step(ins)
                dve.wait_ge(ones_set, done[0])

            for t in (dst_i, src_i):
                dve.memset(t[:, :], FAR if t is dst_i else 0)
            dve.memset(prev_i[:, :], -1)
            dve.memset(next_i[:, :], -1)
            chain(dve.drain())
            for t in (WKS, WVS, WQS, WES, WOS):
                dve.memset(t[:, :, :], 0.0)
            dve.memset(vec[:, :], 0.0)
            chain(dve.drain())
            dve.memset(X[:, :, :, :], 0.0)
            chain(dve.drain())
            for t in (EA, S, N0, X2, PAY):
                dve.memset(t[:, :, :, :], 0.0)
            for t in (zero_f, carryT, *heads):
                dve.memset(t[:, :], 0.0)
            chain(dve.drain())
            dve.memset(eps_col, EPS)
            dve.memset(center[:, :], 0.0)
            chain(dve.drain())
            dve.memset(center[0:64, 0:64], -1.0 / D)
            dve.memset(center[64:128, 64:128], -1.0 / D)
            dve.wait_ge(pool_set, 2)
            chain(dve.drain())
            dve.tensor_scalar(out=mean[:, :], in0=center[:, :], scalar1=-1.0, scalar2=None, op0=ALU.mult)
            chain(dve.drain())
            chain(dve.tensor_tensor(out=center[:, :], in0=center[:, :], in1=ident[:, :], op=ALU.add))
            dve.wait_ge(e_loaded, 64)
            chain(dve.tensor_copy(dst_f[:, :], dst_i[:, :]))
            dve.tensor_copy(shift_f[:, 1:ET], dst_f[:, 0:ET - 1])
            dve.tensor_copy(shift_f[:, 0:1], prev_i[:, :])
            chain(dve.drain())
            chain(dve.tensor_tensor(out=cont[:, :], in0=dst_f[:, :], in1=shift_f[:, :], op=ALU.is_equal))
            chain(dve.tensor_tensor_scan(out=head[:, :], data0=cont[:, :], data1=zero_f[:, :], initial=1.0,
                                         op0=ALU.mult, op1=ALU.add))
            dve.tensor_copy(through[:, :], head[:, ET - 1:ET].to_broadcast([128, PW]))
            dve.memset(cont[:, 0:1], 0.0)
            chain(dve.drain())
            chain(dve.tensor_copy(inner[:, :], cont[:, :]))
            dve.tensor_copy(shift_f[:, 0:ET - 1], dst_f[:, 1:ET])
            dve.tensor_copy(shift_f[:, ET - 1:ET], next_i[:, :])
            chain(dve.drain())
            dve.memset(inner[:, :].rearrange("p (u g) -> p u g", g=GP)[:, :, 0:1], 0.0)
            for k, n in enumerate((4, 1)):
                for q in range(2):
                    for m in range(n):
                        dve.tensor_reduce(out=heads[k][:, q * n + m:q * n + m + 1],
                                          in_=ident[:, 64 * q + 64 // n * m:64 * q + 64 // n * (m + 1)], axis=AX.X, op=ALU.add)
            chain(dve.drain())
            for k, n in enumerate((4, 1)):
                dve.tensor_scalar(out=heads[k][:, :], in0=heads[k][:, :], scalar1=float(D // n) ** -0.5, scalar2=None, op0=ALU.mult)
            chain(dve.tensor_tensor(out=far_f[:, :], in0=dst_f[:, :], in1=shift_f[:, :], op=ALU.is_equal))
            chain(dve.scalar_tensor_tensor(out=far_f[:, :], in0=far_f[:, :], scalar=float(FAR), in1=dst_f[:, :],
                                           op0=ALU.mult, op1=ALU.add))
            dve.tensor_copy(sidx[:, :], far_f[:, :])
            dve.tensor_copy(gidx[:, :, 0:GP], src_i[:, :].rearrange("p (u g) -> p u g", g=GP))
            chain(dve.tensor_scalar(out=dst_f[:, :], in0=dst_f[:, :], scalar1=float(N - 1), scalar2=None, op0=ALU.min))
            dve.tensor_copy(gidx[:, :, GP:2 * GP], dst_f[:, :].rearrange("p (u g) -> p u g", g=GP))
            dve.drain().then_inc(idx_ready, 1)
            dve.wait_ge(w_loaded, 16 * N_W)
            dve.wait_ge(m_loaded, 16 * N_M)
            dve.wait_ge(w_turned, 3)
            for q in range(2):
                p = slice(64 * q, 64 * q + 64)
                dve.tensor_copy(w_v[2][p, p], banks[p, 1, 0:64])
                dve.tensor_copy(w_q[2][p, p], banks[p, 0, 0:64])
                dve.tensor_copy(w_o[2][p, p], banks[p, 2, 0:64])
            dve.drain().then_inc(w_taken, 1)
            for l in range(2):
                dve.tensor_tensor(out=col(f"y{l}"), in0=col(f"s1{l}"), in1=col(f"b2{l}"), op=ALU.add)
                dve.tensor_scalar(out=center_1[l][:, :], in0=center[:, :], scalar1=col(f"g1{l}"), scalar2=None, op0=ALU.mult)
            dve.tensor_scalar(out=center_in[:, :], in0=center[:, :], scalar1=col("g20"), scalar2=None, op0=ALU.mult)
            dve.tensor_tensor(out=col("in1"), in0=col("s20"), in1=col("bO1"), op=ALU.add)
            dve.wait_ge(w_turned, 6)
            for l in range(2):
                dve.tensor_tensor(out=col(f"fb{l}"), in0=col(f"fb{l}"), in1=banks[:, 4 + l, 0:1], op=ALU.add)
            dve.tensor_tensor(out=col("obf"), in0=col("ob"), in1=banks[:, 6, 0:1], op=ALU.add)
            dve.tensor_copy(throughT[:, :], banks[0:PW, 7, 0:128])
            for l in range(2):
                dve.tensor_scalar(out=w_1[l][:, :], in0=w_1[l][:, :], scalar1=col(f"g1{l}"), scalar2=None, op0=ALU.mult)
            dve.drain().then_inc(w_taken, 1)
            for l in range(3):
                for q in range(2):
                    p = slice(64 * q, 64 * q + 64)
                    dve.tensor_reduce(out=wsum[p, l:l + 1], in_=w_o[l][p, p], axis=AX.X, op=ALU.add)
            for l in range(2):
                dve.tensor_reduce(out=wsum[:, 3 + l:4 + l], in_=w_2[l][:, :], axis=AX.X, op=ALU.add)
            chain(dve.drain())
            chain(dve.tensor_scalar(out=wsum[:, 0:5], in0=wsum[:, 0:5], scalar1=1.0 / D, scalar2=None, op0=ALU.mult))
            for l in range(3):
                for q in range(2):
                    p = slice(64 * q, 64 * q + 64)
                    dve.tensor_scalar(out=w_o[l][p, p], in0=w_o[l][p, p], scalar1=wsum[p, l:l + 1], scalar2=None,
                                      op0=ALU.subtract)
            for l in range(2):
                dve.tensor_scalar(out=w_2[l][:, :], in0=w_2[l][:, :], scalar1=wsum[:, 3 + l:4 + l], scalar2=None,
                                  op0=ALU.subtract)
            dve.wait_ge(w_turned, 7)
            for k, name in enumerate(CENTRED):
                dve.tensor_copy(col(CENTRED[name]), banks[:, 0, k:k + 1])
            dve.drain().then_inc(prep, 1)
            dve.wait_ge(prep, 4)

            def sum_x(ph, u):
                g, h = wide[ph], u.slot
                w(dve, x_loaded.done(ph, u))
                dve.tensor_reduce(out=st0[:, h, 0, 0:g], in_=X[:, h, 0:g, :], axis=AX.X, op=ALU.add
                    ).then_inc(x_summed.sem, 1)

            def front_a(ph, u):
                g, h = wide[ph], u.slot
                sum_x(ph, u)
                w(dve, x_summed.done(ph, u))
                dve.scalar_tensor_tensor(out=XM[:, h, 0:g, :], in0=st0[:, h, 0, 0:g].unsqueeze(2).to_broadcast([128, g, D]),
                                         scalar=-1.0 / D, in1=X[:, h, 0:g, :], op0=ALU.mult, op1=ALU.add
                                         ).then_inc(x_centred.sem, 1)

            def squares0(ph, u):
                g, h = wide[ph], u.slot
                w(dve, x_squared.done(ph, u))
                dve.tensor_reduce(out=st0[:, h, 1, 0:g], in_=SQ0[:, h, 0:g, :], axis=AX.X, op=ALU.add
                    ).then_inc(x_squares_summed.sem, 1)

            def norm_x(ph, u):
                g, h = wide[ph], u.slot
                w(dve, x_rstd_ready.done(ph, u))
                w(dve, rows_turned.before(ph, u))
                dve.scalar_tensor_tensor(out=N0[:, h, 0:g, :], in0=XM[:, h, 0:g, :], scalar=0.0,
                                         in1=st0[:, h, 3, 0:g].unsqueeze(2).to_broadcast([128, g, D]),
                                         op0=ALU.max, op1=ALU.mult).then_inc(x_normed.sem, 1)

            def h_turned(ph, u):
                w(dve, rows_turned.done(ph, u))
                to = HT[:, u.slot, 0, :, :].rearrange("p j n -> p (j n)")
                if ph in FIX and ph[1] != 1:
                    ins = dve.tensor_scalar(out=to, in0=psT[u.slot], scalar1=0.0, scalar2=None, op0=ALU.max)
                else:
                    ins = dve.tensor_copy(to, psT[u.slot])
                ins.then_inc(turned_rows_kept.sem, 1)

            def norm1(ph, u):
                h = u.slot
                w(dve, rstd_ready.done(ph, u))
                if ph not in FFN:
                    w(dve, out_kept.before(ph, u))
                dve.scalar_tensor_tensor(out=NT[:, h, :], in0=psC[h], scalar=shift1(ph), in1=R1[:, h, :],
                                         op0=ALU.add, op1=ALU.mult).then_inc(normed_before_net.sem, 1)

            def free_out(ph, u):
                if ph[0] == "dense":
                    w(dve, rows_stored.before(ph, u))
                else:
                    dve.wait_ge(scattered.sems[u.slot], GP * scattered.base[ph][u.slot] + 16 * GP * u.turn)
                    dve.tensor_copy(IB[:, u.slot, 0:GP], sidx[:, bass.ds(u.n * GP, GP)]).then_inc(scatter_idx_ready.sem, 1)

            def squares2(ph, u):
                w(dve, out_squared.done(ph, u))
                dve.tensor_reduce(out=st2[:, u.slot, 1, :], in_=SQ2[:, u.slot, :, :], axis=AX.X, op=ALU.add
                    ).then_inc(out_squares_summed.sem, 1)

            def norm2(ph, u):
                h = u.slot
                w(dve, out_rstd_ready.done(ph, u))
                if ph not in BACK:
                    free_out(ph, u)
                dve.tensor_tensor(out=N2[:, h, :, :], in0=rows8(psN),
                                  in1=st2[:, h, 3, :].unsqueeze(2).to_broadcast([128, GP, D]), op=ALU.mult
                                  ).then_inc(out_normed.sem, 1)

            def residual(ph, u):
                h = u.slot
                w(dve, residual_loaded.done(ph, u))
                if ph in P1:
                    w(dve, out_normed.done(ph, u))
                    dve.tensor_tensor(out=NG[:, :, :], in0=N2[:, h, :, :],
                                      in1=gain_row[:, :].unsqueeze(1).to_broadcast([128, GP, D]), op=ALU.mult
                                          ).then_inc(gain_applied.sem, 1)
                    dve.tensor_tensor(out=XS[:, :, :], in0=X2[:, h, :, :],
                                      in1=shift_row[:, :].unsqueeze(1).to_broadcast([128, GP, D]), op=ALU.add
                                          ).then_inc(residual_shifted.sem, 1)
                    w(dve, residual_shifted.done(ph, u))
                    free_out(ph, u)
                    ins = dve.tensor_tensor(out=OUT[:, h, :, :], in0=NG[:, :, :], in1=XS[:, :, :], op=ALU.add)
                else:
                    w(dve, out_turned.done(ph, u))
                    free_out(ph, u)
                    ins = dve.tensor_tensor(out=OUT[:, h, :, :], in0=rows8(psN), in1=X2[:, h, :, :], op=ALU.add)
                ins.then_inc(residual_added.sem, 1)

            def whole_sums(ph, u):
                h, hh = u.slot, HEADS[ph[1]]
                dve.tensor_copy(CB[:, h, :], head[:, bass.ds(u.n * GP, GP)]).then_inc(heads_copied.sem, 1)
                w(dve, heads_copied.done(ph, u))
                w(dve, sums_loaded.done(ph, u))
                for g in range(GP):
                    ins = dve.scalar_tensor_tensor(out=T[:, h, 0:D + hh, g], in0=carry[:, 0:D + hh], scalar=CB[:, h, g:g + 1],
                                                   in1=SIN[:, h, 0:D + hh, g], op0=ALU.mult, op1=ALU.add)
                ins.then_inc(whole_sums_ready.sem, 1)

            def attention(ph, u):
                h, hh = u.slot, HEADS[ph[1]]
                w(dve, whole_sums_ready.done(ph, u))
                z = [ZR[:, h, k, 0:hh, :] for k in range(2)]
                dve.tensor_scalar(out=z[0], in0=T[:, h, D:D + hh, :], scalar1=ZEPS if ph[1] < 2 else 0.0, scalar2=None,
                                  op0=ALU.add).then_inc(weight_sums_ready.sem, 1)
                w(dve, weight_sums_ready.done(ph, u))
                dve.reciprocal(out=z[1], in_=z[0]).then_inc(weight_sums_inverted.sem, 1)
                w(dve, weight_sums_inverted.done(ph, u))
                w(dve, attention_in_psum.before(ph, u))
                dve.tensor_tensor(out=ATT[:, h, :, :].rearrange("p g (k d) -> p g k d", k=hh),
                                  in0=T[:, h, 0:D, :].rearrange("p (k d) g -> p g k d", k=hh),
                                  in1=z[1].rearrange("p k g -> p g k").unsqueeze(3).to_broadcast([128, GP, hh, D // hh]),
                                  op=ALU.mult).then_inc(attention_ready.sem, 1)

            def update(ph):
                def last_layer(at):
                    for u in at(3):
                        squares0(ph, u)
                    for u in at(2):
                        h_turned(ph, u)
                    for u in at(4):
                        front_a(ph, u)
                    for u in at(3):
                        norm_x(ph, u)
                    for u in at(0):
                        residual(ph, u)
                    for u in at(1):
                        norm1(ph, u)

                def body(at):
                    if ph in RAW:
                        for u in at(2):
                            squares0(ph, u)
                        for u in at(3):
                            front_a(ph, u)
                    if ph in FIX:
                        for u in at(3):
                            whole_sums(ph, u)
                    if ph in FFN:
                        for u in at(-1):
                            squares2(ph, u)
                    if ph in FIX:
                        for u in at(3):
                            attention(ph, u)
                    if ph in RAW:
                        for u in at(2):
                            norm_x(ph, u)
                    if ph in FFN:
                        for u in at(-1):
                            norm2(ph, u)
                    else:
                        for u in at(0):
                            residual(ph, u)
                    for u in at(2):
                        h_turned(ph, u)
                    for u in at(1):
                        norm1(ph, u)
                    if ph in P1:
                        for u in at(-1):
                            residual(ph, u)
                return last_layer if ph == ("dense", 2) else body

            def edges(ph):
                l = ph[1]
                hh = HEADS[l]

                def products(u):
                    w(dve, queries_kept.done(ph, u))
                    w(dve, keys_ready.done(ph, u))
                    if l == 2:
                        dve.scalar_tensor_tensor(out=PR[:, :], in0=psK, scalar=col("qkb"), in1=QS[:, :], op0=ALU.add,
                                                 op1=ALU.mult).then_inc(key_query_ready.sem, 1)
                        return
                    dve.tensor_tensor(out=PR[:, :], in0=psK, in1=QS[:, :], op=ALU.mult).then_inc(key_query_ready.sem, 1)
                    w(dve, key_query_ready.done(ph, u))
                    w(dve, edge_factors_ready.done(ph, u))
                    dve.tensor_tensor(out=PR2[:, :], in0=psE, in1=PR[:, :], op=ALU.mult).then_inc(factors_ready.sem, 1)

                def clip(u):
                    w(dve, scores_ready.done(ph, u))
                    dve.tensor_scalar(out=SC[:, 0:GP * hh], in0=psS[:, 0:GP * hh], scalar1=5.0, scalar2=-5.0,
                                      op0=ALU.min, op1=ALU.max).then_inc(scores_clipped.sem, 1)

                def message(u):
                    h = u.slot
                    w(dve, weights_ready.done(ph, u))
                    w(dve, values_ready.done(ph, u))
                    dve.tensor_tensor(out=PAY[:, h, 0:D, :].rearrange("p (k d) g -> p g k d", k=hh),
                                      in0=psV.rearrange("p (g k d) -> p g k d", k=hh, d=D // hh),
                                      in1=PAY[:, h, D:D + hh, :].rearrange("p k g -> p g k").unsqueeze(3)
                                      .to_broadcast([128, GP, hh, D // hh]), op=ALU.mult).then_inc(messages_ready.sem, 1)

                def go_on(u):
                    h = u.slot
                    w(dve, messages_ready.done(ph, u))
                    w(dve, flags_spread.done(ph, u))
                    dve.scalar_tensor_tensor(out=PAY[:, h, 0:D + hh, 0], in0=S[:, 1 - h, 0:D + hh, GP - 1], scalar=CB[:, h, 0:1],
                                             in1=PAY[:, h, 0:D + hh, 0], op0=ALU.mult, op1=ALU.add
                                                 ).then_inc(carried_on.sem, 1)

                def sums_of(u):
                    h = u.slot
                    w(dve, carried_on.done(ph, u))
                    w(dve, sums_stored.before(ph, u))
                    flat_ = [b[:, h, 0:D + hh, :].rearrange("p c g -> p (c g)") for b in (S, FL, PAY)]
                    dve.tensor_tensor_scan(out=flat_[0], data0=flat_[1], data1=flat_[2], initial=0.0,
                                           op0=ALU.mult, op1=ALU.add).then_inc(sums_ready.sem, 1)

                def body(at):
                    for u in at(-1):
                        clip(u)
                    if ph in RAW:
                        for u in at(3):
                            sum_x(ph, u)
                    for u in at(-1):
                        message(u)
                    if ph in RAW:
                        for u in at(2):
                            squares0(ph, u)
                    for u in at(0):
                        products(u)
                    for u in at(-1):
                        go_on(u)
                        sums_of(u)
                return body

            def carry_over(l):
                hh = HEADS[l]
                dve.wait_ge(last_sums_turned, l + 1)
                dve.tensor_tensor_scan(out=carryT[0:D + hh, 1:129], data0=throughT[0:D + hh, :],
                                       data1=banks[0:D + hh, 0, 0:128], initial=0.0, op0=ALU.mult, op1=ALU.add
                                       ).then_inc(carry_scanned, 1)
                dve.wait_ge(carry_turned, l + 1)
                dve.tensor_copy(carry[:, 0:D + hh], banks[:, 1, 0:D + hh]).then_inc(carry_ready, 1)
                dve.wait_ge(carry_ready, l + 1)

            for ph in PHASES:
                if ph[0] == "fix":
                    carry_over(ph[1])
                if ph[0] == "edge":
                    periods(dve, units(ph), -1, 3, edges(ph))
                else:
                    periods(dve, units(ph), -1, 4, update(ph))
                barrier(dve, ph)

        @block.tensor
        def _(pe):
            for c in owner["pe"]:
                pe.sem_inc(c.sem, 2)
            pe.wait_ge(w_loaded, 16 * N_W)
            pe.wait_ge(m_loaded, 16 * N_M)
            pe.wait_ge(pool_set, 2)
            pe.wait_ge(idx_ready, 1)
            for k in range(3):
                pe.transpose(banks[:, k, 0:64], wtmp[:, k, :], ident[0:64, 0:64]).then_inc(w_turned, 1)
            pe.wait_ge(w_taken, 1)
            for l in range(2):
                ins = pe.matmul(banks[:, 4 + l, 0:1], w_1[l][0:64, :], col(f"s1{l}")[0:64, :], start=True, stop=True)
            ins.then_inc(w_turned, 1)
            for q in range(2):
                p = slice(64 * q, 64 * q + 64)
                ins = pe.matmul(banks[p, 6, 0:1], w_o[2][:, p], col("vb"), start=True, stop=True)
            ins.then_inc(w_turned, 1)
            pe.transpose(banks[0:PW, 7, 0:128], through[:, :], ident[:, :]).then_inc(w_turned, 1)
            pe.wait_ge(w_taken, 2)
            for k, name in enumerate(CENTRED):
                ins = pe.matmul(banks[:, 0, k:k + 1], center[:, :], col(name), start=True, stop=True)
            ins.then_inc(w_turned, 1)
            pe.drain().then_inc(prep, 1)
            pe.wait_ge(prep, 4)

            def turn(to, rows, h, g0=0):
                for j in range(4):
                    ins = pe.transpose(to[:, 128 * j:128 * j + 128],
                                       rows[:, h, g0 + 2 * j:g0 + 2 * j + 2, :].rearrange("p g d -> p (g d)"), ident[:, :])
                return ins

            def flat(buf, h):
                return buf[:, h, :, :].rearrange("p j n -> p (j n)")

            def tp_in(ph, u):
                w(pe, (x_normed if ph in RAW else rows_loaded).done(ph, u))
                if ph == ("dense", 2):
                    w(pe, variance_logged.before(ph, u))
                turn(psT[u.slot], N0, u.slot).then_inc(rows_turned.sem, 1)

            def tp_att(ph, u):
                w(pe, attention_ready.done(ph, u))
                turn(psC[u.slot], ATT, u.slot).then_inc(attention_in_psum.sem, 1)

            def centred(ph, u):
                w(pe, turned_rows_kept.done(ph, u))
                fixed = ph in FIX
                if fixed:
                    w(pe, attention_kept.done(ph, u))
                ins = pe.matmul(psC[u.slot], (center_in if ph[1] == 1 else center)[:, :],
                                HT[:, u.slot, 0, :, :].rearrange("p j n -> p (j n)"), start=True, stop=not fixed)
                if fixed:
                    ins = pe.matmul(psC[u.slot], w_o[ph[1]][:, :], flat(ATTT, u.slot), start=False, stop=True)
                ins.then_inc(centred_ready.sem, 1)

            def variance(ph, u):
                w(pe, centred_squared.done(ph, u))
                pe.matmul(psT[u.slot], mean[:, :], SQ1[:, u.slot, :], start=True, stop=True).then_inc(variance_ready.sem, 1)

            def hidden(ph, u):
                w(pe, normed_before_net.done(ph, u))
                for q in range(2):
                    p = slice(64 * q, 64 * q + 64)
                    pe.matmul(psH[q], w_1[ph[1]][p, :], NT[p, u.slot, :], start=True, stop=True
                        ).then_inc(hidden_in_psum[q].sem, 1)

            def net_out(ph, u):
                pe.matmul(psZ, center_1[ph[1]][:, :], NT[:, u.slot, :], start=True, stop=True)
                w(pe, hidden_ready.done(ph, u))
                for q in range(2):
                    p = slice(64 * q, 64 * q + 64)
                    ins = pe.matmul(psZ[p, :], w_2[ph[1]][:, :], HID[:, q, :], start=False, stop=True, skip_group_check=True)
                ins.then_inc(net_ready.sem, 1)

            def to_rows(ph, u):
                w(pe, out_kept.done(ph, u))
                w(pe, (out_normed if ph in FFN else residual_added).before(ph, u, 1))
                for j in range(4):
                    ins = pe.transpose(psN[:, 128 * j:128 * j + 128], ZT[:, u.slot, j, :], ident[:, :])
                ins.then_inc(out_turned.sem, 1)

            def update(ph):
                def last_layer(at):
                    for u in at(1):
                        centred(ph, u)
                    for u in at(2):
                        tp_in(ph, u)
                    for u in at(1):
                        variance(ph, u)
                    for u in at(0):
                        to_rows(ph, u)

                def body(at):
                    for u in at(1):
                        centred(ph, u)
                    if ph in FFN:
                        for u in at(-1):
                            to_rows(ph, u)
                        for u in at(0):
                            hidden(ph, u)
                    else:
                        for u in at(0):
                            to_rows(ph, u)
                    for u in at(1):
                        variance(ph, u)
                    for u in at(2):
                        tp_in(ph, u)
                        if ph in FIX:
                            tp_att(ph, u)
                    if ph in FFN:
                        for u in at(0):
                            net_out(ph, u)
                return last_layer if ph == ("dense", 2) else body

            def edges(ph):
                l = ph[1]
                hh = HEADS[l]
                sel = heads[1 if l == 2 else 0]

                def turn_ends(u):
                    h = u.slot
                    w(pe, (x_normed if ph in RAW else rows_loaded).done(ph, u))
                    turn(psX[0], N0, h)
                    ins = turn(psX[1], N0, h, GP)
                    if l < 2:
                        w(pe, edge_rows_loaded.done(ph, u))
                        ins = turn(psX[2], EA, h)
                    ins.then_inc(ends_in_psum.sem, 1)

                def keys(u):
                    w(pe, targets_kept.done(ph, u))
                    pe.matmul(psQ, w_q[l][:, :], flat(HT[:, :, 1, :, :], u.slot), start=True, stop=True
                        ).then_inc(queries_ready.sem, 1)
                    w(pe, sources_kept.done(ph, u))
                    pe.matmul(psK, (w_k[l] if l < 2 else w_q[2])[:, :], flat(HT[:, :, 0, :, :], u.slot), start=True, stop=True
                              ).then_inc(keys_ready.sem, 1)
                    if l < 2:
                        w(pe, edge_rows_kept.done(ph, u))
                        pe.matmul(psE, w_e[l][:, :], flat(EAT, u.slot), start=True, stop=True
                            ).then_inc(edge_factors_ready.sem, 1)

                def values(u):
                    w(pe, messages_ready.before(ph, u, 1))
                    for j in range(4):
                        ins = pe.matmul(psV[:, 128 * j:128 * j + 128], HT[:, u.slot, 0, j, :], w_v[l][:, :], start=True, stop=True)
                    ins.then_inc(values_ready.sem, 1)

                def scores(u):
                    w(pe, (factors_ready if l < 2 else key_query_ready).done(ph, u))
                    w(pe, scores_clipped.before(ph, u, 1))
                    for j in range(4):
                        ins = pe.matmul(psS[:, 2 * hh * j:2 * hh * (j + 1)], (PR2 if l < 2 else PR)[:, 128 * j:128 * j + 128],
                                        sel[:, :], start=True, stop=True)
                    ins.then_inc(scores_ready.sem, 1)

                def body(at):
                    for u in at(0):
                        keys(u)
                    for u in at(1):
                        turn_ends(u)
                    for u in at(0):
                        values(u)
                        scores(u)
                return body

            for ph in PHASES:
                if ph[0] == "fix":
                    hh = HEADS[ph[1]]
                    pe.transpose(banks[0:D + hh, 0, 0:128], S[:, (EUNITS - 1) % 2, 0:D + hh, GP - 1], ident[:, :]
                        ).then_inc(last_sums_turned, 1)
                    pe.wait_ge(carry_scanned, ph[1] + 1)
                    pe.transpose(banks[:, 1, 0:D + hh], carryT[0:D + hh, 0:128], ident[0:D + hh, 0:D + hh]
                        ).then_inc(carry_turned, 1)
                    pe.wait_ge(carry_ready, ph[1] + 1)
                if ph[0] == "edge":
                    periods(pe, units(ph), 0, 1, edges(ph))
                else:
                    periods(pe, units(ph), -1, 2, update(ph))
                barrier(pe, ph)


_INS = ['x', 'src', 'dst', 'edge_attr_64', 'L0_gnn_WQ', 'L0_gnn_WK', 'L0_gnn_WE', 'L0_gnn_WV', 'L0_gnn_WO', 'L0_gnn_bO',
        'L0_gnn_ln1_g', 'L0_gnn_ln1_b', 'L0_gnn_W1', 'L0_gnn_b1', 'L0_gnn_W2', 'L0_gnn_b2', 'L0_gnn_ln2_g', 'L0_gnn_ln2_b',
        'L1_gnn_qk_w', 'L1_gnn_qk_b', 'L1_gnn_v_w', 'L1_gnn_v_b', 'L1_gnn_o_w', 'L1_gnn_o_b', 'L1_gnn_ln_g', 'L1_gnn_ln_b']


def kernel(**inputs):
    import numpy as _np
    import concourse.bacc as _bacc
    from concourse import mybir as _mybir
    from concourse.bass_utils import run_bass_kernel_spmd as _run

    nc = _bacc.Bacc("TRN2", target_bir_lowering=False, num_devices=1)
    arrays, args = {}, []
    for name in _INS:
        a = _np.ascontiguousarray(inputs[name])
        arrays[f"in_{name}_dram"] = a
        args.append(nc.dram_tensor(f"in_{name}_dram", a.shape, _mybir.dt.from_np(a.dtype), kind="ExternalInput").ap())
    args.append(nc.dram_tensor("out_0_dram", (N, D), _mybir.dt.float32, kind="ExternalOutput").ap())
    build(nc, *args)
    r = _run(nc, [arrays], core_ids=[0])
    return r.results[0]["out_0_dram"]
```
